# Optimizing a Trainium2 kernel written in Bass

```python
import numpy as np
import jax
import jax.numpy as jnp

def _softmax(x, axis=-1):
    return jax.nn.softmax(x, axis=axis)

def _gelu(x):
    return jax.nn.gelu(x, approximate=True)

def _silu(x):
    return jax.nn.silu(x)

def _sigmoid(x):
    return jax.nn.sigmoid(x)

def _layernorm(x, axis=-1, eps=1e-05):
    m = jnp.mean(x, axis=axis, keepdims=True)
    v = jnp.var(x, axis=axis, keepdims=True)
    return (x - m) / jnp.sqrt(v + eps)

def _scatter_add(tgt, idx, src, axis=0):
    return tgt.at[idx].add(src)

def _segment_sum(src, seg, n):
    return jax.ops.segment_sum(src, seg, n)
kernel_name = 'mk_dlrm_tower_d1_rec_r8_a5d795'

def setup_inputs(seed: int=0):
    np.random.seed(seed)
    _w = jnp.asarray

    def _rec_inputs():
        import jax
        import jax.numpy as jnp
        _tk = jax.random.key(seed)
        dense_ctx = jax.random.normal(jax.random.fold_in(_tk, 190), (1024, 16), jnp.float32)
        ids = jnp.stack([jax.random.randint(jax.random.fold_in(_tk, 200 + f), (1024,), 0, v, jnp.int32) for f, v in enumerate([12500, 125000, 1250, 125000, 1000, 12500, 1000, 125000, 1000, 12500, 1250, 1250, 1250, 1000, 12500, 1000, 1000, 12500, 1000, 1250, 1000, 1250, 1250, 1250, 1000, 1000, 1000, 1250, 12500, 1000, 1250, 1250])], axis=1)
        tbl_0 = 0.05 * jax.random.normal(jax.random.fold_in(_tk, 500 + 0), (12500, 64), jnp.float32)
        tbl_1 = 0.05 * jax.random.normal(jax.random.fold_in(_tk, 500 + 1), (125000, 64), jnp.float32)
        tbl_2 = 0.05 * jax.random.normal(jax.random.fold_in(_tk, 500 + 2), (1250, 64), jnp.float32)
        tbl_3 = 0.05 * jax.random.normal(jax.random.fold_in(_tk, 500 + 3), (125000, 64), jnp.float32)
        tbl_4 = 0.05 * jax.random.normal(jax.random.fold_in(_tk, 500 + 4), (1000, 64), jnp.float32)
        tbl_5 = 0.05 * jax.random.normal(jax.random.fold_in(_tk, 500 + 5), (12500, 64), jnp.float32)
        tbl_6 = 0.05 * jax.random.normal(jax.random.fold_in(_tk, 500 + 6), (1000, 64), jnp.float32)
        tbl_7 = 0.05 * jax.random.normal(jax.random.fold_in(_tk, 500 + 7), (125000, 64), jnp.float32)
        tbl_8 = 0.05 * jax.random.normal(jax.random.fold_in(_tk, 500 + 8), (1000, 64), jnp.float32)
        tbl_9 = 0.05 * jax.random.normal(jax.random.fold_in(_tk, 500 + 9), (12500, 64), jnp.float32)
        tbl_10 = 0.05 * jax.random.normal(jax.random.fold_in(_tk, 500 + 10), (1250, 64), jnp.float32)
        tbl_11 = 0.05 * jax.random.normal(jax.random.fold_in(_tk, 500 + 11), (1250, 64), jnp.float32)
        tbl_12 = 0.05 * jax.random.normal(jax.random.fold_in(_tk, 500 + 12), (1250, 64), jnp.float32)
        tbl_13 = 0.05 * jax.random.normal(jax.random.fold_in(_tk, 500 + 13), (1000, 64), jnp.float32)
        tbl_14 = 0.05 * jax.random.normal(jax.random.fold_in(_tk, 500 + 14), (12500, 64), jnp.float32)
        tbl_15 = 0.05 * jax.random.normal(jax.random.fold_in(_tk, 500 + 15), (1000, 64), jnp.float32)
        tbl_16 = 0.05 * jax.random.normal(jax.random.fold_in(_tk, 500 + 16), (1000, 64), jnp.float32)
        tbl_17 = 0.05 * jax.random.normal(jax.random.fold_in(_tk, 500 + 17), (12500, 64), jnp.float32)
        tbl_18 = 0.05 * jax.random.normal(jax.random.fold_in(_tk, 500 + 18), (1000, 64), jnp.float32)
        tbl_19 = 0.05 * jax.random.normal(jax.random.fold_in(_tk, 500 + 19), (1250, 64), jnp.float32)
        tbl_20 = 0.05 * jax.random.normal(jax.random.fold_in(_tk, 500 + 20), (1000, 64), jnp.float32)
        tbl_21 = 0.05 * jax.random.normal(jax.random.fold_in(_tk, 500 + 21), (1250, 64), jnp.float32)
        tbl_22 = 0.05 * jax.random.normal(jax.random.fold_in(_tk, 500 + 22), (1250, 64), jnp.float32)
        tbl_23 = 0.05 * jax.random.normal(jax.random.fold_in(_tk, 500 + 23), (1250, 64), jnp.float32)
        tbl_24 = 0.05 * jax.random.normal(jax.random.fold_in(_tk, 500 + 24), (1000, 64), jnp.float32)
        tbl_25 = 0.05 * jax.random.normal(jax.random.fold_in(_tk, 500 + 25), (1000, 64), jnp.float32)
        tbl_26 = 0.05 * jax.random.normal(jax.random.fold_in(_tk, 500 + 26), (1000, 64), jnp.float32)
        tbl_27 = 0.05 * jax.random.normal(jax.random.fold_in(_tk, 500 + 27), (1250, 64), jnp.float32)
        tbl_28 = 0.05 * jax.random.normal(jax.random.fold_in(_tk, 500 + 28), (12500, 64), jnp.float32)
        tbl_29 = 0.05 * jax.random.normal(jax.random.fold_in(_tk, 500 + 29), (1000, 64), jnp.float32)
        tbl_30 = 0.05 * jax.random.normal(jax.random.fold_in(_tk, 500 + 30), (1250, 64), jnp.float32)
        tbl_31 = 0.05 * jax.random.normal(jax.random.fold_in(_tk, 500 + 31), (1250, 64), jnp.float32)
        _rk = jax.random.fold_in(_tk, 7)
        W_top1 = 0.0693375 * jax.random.normal(jax.random.fold_in(_tk, 801), (208, 512), jnp.float32)
        W_top2 = 0.0441942 * jax.random.normal(jax.random.fold_in(_tk, 802), (512, 256), jnp.float32)
        W_top3 = 0.0625 * jax.random.normal(jax.random.fold_in(_tk, 803), (256, 1), jnp.float32)
        b_top1 = jnp.zeros((512,), jnp.float32)
        b_top2 = jnp.zeros((256,), jnp.float32)
        return (dense_ctx, ids, tbl_0, tbl_1, tbl_2, tbl_3, tbl_4, tbl_5, tbl_6, tbl_7, tbl_8, tbl_9, tbl_10, tbl_11, tbl_12, tbl_13, tbl_14, tbl_15, tbl_16, tbl_17, tbl_18, tbl_19, tbl_20, tbl_21, tbl_22, tbl_23, tbl_24, tbl_25, tbl_26, tbl_27, tbl_28, tbl_29, tbl_30, tbl_31, W_top1, b_top1, W_top2, b_top2, W_top3)
    dense_ctx, ids, tbl_0, tbl_1, tbl_2, tbl_3, tbl_4, tbl_5, tbl_6, tbl_7, tbl_8, tbl_9, tbl_10, tbl_11, tbl_12, tbl_13, tbl_14, tbl_15, tbl_16, tbl_17, tbl_18, tbl_19, tbl_20, tbl_21, tbl_22, tbl_23, tbl_24, tbl_25, tbl_26, tbl_27, tbl_28, tbl_29, tbl_30, tbl_31, W_top1, b_top1, W_top2, b_top2, W_top3 = _rec_inputs()

    def _L0_rec_setup():
        import jax, jax.numpy as jnp
        import numpy as np
        B, F, D = (256, 32, 64)
        LAYER_SIZE = (128, 128)

        def _cin_layer(h, x0, W, b):
            bsz, H, d = h.shape
            M = x0.shape[1]
            z = jnp.einsum('bhd,bmd->bhmd', h, x0).reshape(bsz, H * M, d)
            out = jnp.einsum('bcd,oc->bod', z, W) + b[None, :, None]
            return jax.nn.relu(out)
        key = jax.random.key(seed)
        k1, k2, k3 = jax.random.split(key, 3)
        inputs = jax.random.normal(k1, (B, F, D), dtype=jnp.float32)
        W0 = jax.random.normal(k2, (LAYER_SIZE[0], F * F), dtype=jnp.float32) * 0.03
        b0 = jnp.zeros((LAYER_SIZE[0],), dtype=jnp.float32)
        W1 = jax.random.normal(k3, (LAYER_SIZE[1], LAYER_SIZE[0] // 2 * F), dtype=jnp.float32) * 0.03
        b1 = jnp.zeros((LAYER_SIZE[1],), dtype=jnp.float32)
        return {'inputs': inputs, 'W0': W0, 'b0': b0, 'W1': W1, 'b1': b1}
    _L0_rec_all = _L0_rec_setup()
    _L0_rec_in = {k: v for k, v in _L0_rec_all.items() if k in ('W0', 'b0', 'W1', 'b1')}
    del _L0_rec_all
    return {'dense_ctx': dense_ctx, 'ids': ids, 'tbl_0': tbl_0, 'tbl_1': tbl_1, 'tbl_2': tbl_2, 'tbl_3': tbl_3, 'tbl_4': tbl_4, 'tbl_5': tbl_5, 'tbl_6': tbl_6, 'tbl_7': tbl_7, 'tbl_8': tbl_8, 'tbl_9': tbl_9, 'tbl_10': tbl_10, 'tbl_11': tbl_11, 'tbl_12': tbl_12, 'tbl_13': tbl_13, 'tbl_14': tbl_14, 'tbl_15': tbl_15, 'tbl_16': tbl_16, 'tbl_17': tbl_17, 'tbl_18': tbl_18, 'tbl_19': tbl_19, 'tbl_20': tbl_20, 'tbl_21': tbl_21, 'tbl_22': tbl_22, 'tbl_23': tbl_23, 'tbl_24': tbl_24, 'tbl_25': tbl_25, 'tbl_26': tbl_26, 'tbl_27': tbl_27, 'tbl_28': tbl_28, 'tbl_29': tbl_29, 'tbl_30': tbl_30, 'tbl_31': tbl_31, 'W_top1': W_top1, 'b_top1': b_top1, 'W_top2': W_top2, 'b_top2': b_top2, 'W_top3': W_top3, 'L0_rec_W0': _L0_rec_in['W0'], 'L0_rec_b0': _L0_rec_in['b0'], 'L0_rec_W1': _L0_rec_in['W1'], 'L0_rec_b1': _L0_rec_in['b1']}

def reference(dense_ctx, ids, tbl_0, tbl_1, tbl_2, tbl_3, tbl_4, tbl_5, tbl_6, tbl_7, tbl_8, tbl_9, tbl_10, tbl_11, tbl_12, tbl_13, tbl_14, tbl_15, tbl_16, tbl_17, tbl_18, tbl_19, tbl_20, tbl_21, tbl_22, tbl_23, tbl_24, tbl_25, tbl_26, tbl_27, tbl_28, tbl_29, tbl_30, tbl_31, W_top1, b_top1, W_top2, b_top2, W_top3, L0_rec_W0, L0_rec_b0, L0_rec_W1, L0_rec_b1):
    import jax
    import jax.numpy as jnp

    def _L0_rec_ref(inputs, W0, b0, W1, b1):
        import jax, jax.numpy as jnp
        import numpy as np
        B, F, D = (256, 32, 64)
        LAYER_SIZE = (128, 128)

        def _cin_layer(h, x0, W, b):
            bsz, H, d = h.shape
            M = x0.shape[1]
            z = jnp.einsum('bhd,bmd->bhmd', h, x0).reshape(bsz, H * M, d)
            out = jnp.einsum('bcd,oc->bod', z, W) + b[None, :, None]
            return jax.nn.relu(out)
        out0 = _cin_layer(inputs, inputs, W0, b0)
        half = LAYER_SIZE[0] // 2
        next_hidden = out0[:, :half, :]
        direct0 = out0[:, half:, :]
        direct1 = _cin_layer(next_hidden, inputs, W1, b1)
        result = jnp.concatenate([direct0, direct1], axis=1)
        return jnp.sum(result, axis=-1)
    e = jnp.stack([tbl_0[ids[:, 0]], tbl_1[ids[:, 1]], tbl_2[ids[:, 2]], tbl_3[ids[:, 3]], tbl_4[ids[:, 4]], tbl_5[ids[:, 5]], tbl_6[ids[:, 6]], tbl_7[ids[:, 7]], tbl_8[ids[:, 8]], tbl_9[ids[:, 9]], tbl_10[ids[:, 10]], tbl_11[ids[:, 11]], tbl_12[ids[:, 12]], tbl_13[ids[:, 13]], tbl_14[ids[:, 14]], tbl_15[ids[:, 15]], tbl_16[ids[:, 16]], tbl_17[ids[:, 17]], tbl_18[ids[:, 18]], tbl_19[ids[:, 19]], tbl_20[ids[:, 20]], tbl_21[ids[:, 21]], tbl_22[ids[:, 22]], tbl_23[ids[:, 23]], tbl_24[ids[:, 24]], tbl_25[ids[:, 25]], tbl_26[ids[:, 26]], tbl_27[ids[:, 27]], tbl_28[ids[:, 28]], tbl_29[ids[:, 29]], tbl_30[ids[:, 30]], tbl_31[ids[:, 31]]], axis=1)
    z = _L0_rec_ref(e, L0_rec_W0, L0_rec_b0, L0_rec_W1, L0_rec_b1)
    z = z.reshape(z.shape[0], -1)
    h = jnp.concatenate([z, dense_ctx], axis=1)
    h = jnp.maximum(h @ W_top1 + b_top1, 0.0)
    h = jnp.maximum(h @ W_top2 + b_top2, 0.0)
    y = h @ W_top3
    return y

_drawn_inputs = setup_inputs


def setup_inputs(seed=0):
    import zlib

    import numpy as np

    out = dict(_drawn_inputs(seed))
    spreads = {'b_top1': (0.0, 2.0),
     'b_top2': (0.0, 2.0),
     'L0_rec_b0': (0.0, 0.1),
     'L0_rec_b1': (0.0, 0.605)}
    factors = {'tbl_0': 8.0,
     'tbl_1': 8.0,
     'tbl_2': 8.0,
     'tbl_3': 8.0,
     'tbl_4': 8.0,
     'tbl_5': 8.0,
     'tbl_6': 8.0,
     'tbl_7': 8.0,
     'tbl_8': 8.0,
     'tbl_9': 8.0,
     'tbl_10': 8.0,
     'tbl_11': 8.0,
     'tbl_12': 8.0,
     'tbl_13': 8.0,
     'tbl_14': 8.0,
     'tbl_15': 8.0,
     'tbl_16': 8.0,
     'tbl_17': 8.0,
     'tbl_18': 8.0,
     'tbl_19': 8.0,
     'tbl_20': 8.0,
     'tbl_21': 8.0,
     'tbl_22': 8.0,
     'tbl_23': 8.0,
     'tbl_24': 8.0,
     'tbl_25': 8.0,
     'tbl_26': 8.0,
     'tbl_27': 8.0,
     'tbl_28': 8.0,
     'tbl_29': 8.0,
     'tbl_30': 8.0,
     'tbl_31': 8.0,
     'L0_rec_W0': 8.0,
     'L0_rec_W1': 7.944,
     'dense_ctx': 21.377}
    for name, (base, spread) in spreads.items():
        noise = np.random.default_rng([zlib.crc32(name.encode()), seed]).standard_normal(out[name].shape)
        drawn = base * np.exp(spread * noise) if base else spread * noise
        out[name] = jnp.asarray(drawn.astype(out[name].dtype))
    for name, factor in factors.items():
        out[name] = (out[name] * factor).astype(out[name].dtype)
    return out
```

```python
import concourse.bass as bass
from concourse import mybir
from contextlib import ExitStack

VOCABS = [12500, 125000, 1250, 125000, 1000, 12500, 1000, 125000, 1000, 12500, 1250, 1250, 1250, 1000, 12500, 1000,
          1000, 12500, 1000, 1250, 1000, 1250, 1250, 1250, 1000, 1000, 1000, 1250, 12500, 1000, 1250, 1250]
P = 128
B = 1024
F = 32
D = 64
O = 128
HID = 64
CTX = 16
T1 = 512
T2 = 256

BS = 16
N = BS * D
NB = B // BS
BANK = 512
HALVES = N // BANK

R = 4
NT = 4
NHT = 4
UNIT = 2
RING = 5
U0 = NT // UNIT
U1 = NHT * NT // UNIT
US = U0 + U1
HALFTURN = F // 2


def build_tower(nc, table, ids, field_row, half_scale, w0_direct, w0_mirror, w0h_direct, w0h_mirror, w1,
                b0, b1, dense, wtop1, btop1, wtop2, btop2, wtop3, out):
    fp32 = mybir.dt.float32
    i32 = mybir.dt.int32
    ALU = mybir.AluOpType
    ACT = mybir.ActivationFunctionType
    AX = mybir.AxisListType.X

    ctx = ExitStack()
    with ctx:
        def sb(name, shape, dt=fp32):
            return ctx.enter_context(nc.sbuf_tensor(name, shape, dt))

        def pb(name, shape):
            return ctx.enter_context(nc.psum_tensor(name, shape, fp32))

        def sem(name):
            return ctx.enter_context(nc.semaphore(name))

        xs = nc.dram_tensor("xs", [NB, F + HALFTURN, N], fp32).ap()

        ids_sb = sb("ids_sb", [P, NB * 4], i32)
        row_of_field = sb("row_of_field", [P, 1], i32)
        rows = sb("rows", [P, NB * 4], i32)
        idx_now = [sb(f"idx_now{g}", [P, 4], i32) for g in range(2)]
        gathered = [sb(f"gathered{g}", [P, 4 * D]) for g in range(2)]
        base = [sb(f"base{b}", [P, 1, N]) for b in range(2)]
        rot = [sb(f"rot{b}", [P, NT, N]) for b in range(2)]
        lo_half = [sb(f"lo_half{b}", [HALFTURN, N]) for b in range(2)]
        hi_half = [sb(f"hi_half{b}", [HALFTURN, N]) for b in range(2)]
        hid = [sb(f"hid{b}", [P, NHT, N]) for b in range(2)]
        prods = sb("prods", [P, RING * UNIT, N])
        prod = [prods[:, u * UNIT:(u + 1) * UNIT, :] for u in range(RING)]
        prod_half = sb("prod_half", [HALFTURN, N])
        act0 = [sb(f"act0_{b}", [P, N]) for b in range(2)]
        act1 = [sb(f"act1_{b}", [P, N]) for b in range(2)]
        w0_sb = sb("w0_sb", [P, NT, O])
        w0m_sb = sb("w0m_sb", [P, NT, O])
        w0h_sb = sb("w0h_sb", [HALFTURN, O])
        w0hm_sb = sb("w0hm_sb", [HALFTURN, O])
        half_sb = sb("half_sb", [P, 1])
        w1_sb = sb("w1_sb", [P, NHT * NT, O])
        b0_sb = sb("b0_sb", [O, 1])
        b1_sb = sb("b1_sb", [O, 1])
        pooled0 = sb("pooled0", [P, B])
        pooled1 = sb("pooled1", [P, B])
        wt1a = sb("wt1a", [P, T1])
        wt1b = sb("wt1b", [P, T1])
        bt1 = sb("bt1", [P, T1 // P])
        wt2 = sb("wt2", [P, T1 // P, T2])
        bt2 = sb("bt2", [P, T2 // P])
        wt3 = sb("wt3", [P, T2 // P])
        top1 = prods[:, 0:T1 // P, :]
        top2 = prods[:, T1 // P:(T1 + T2) // P, :]
        y_sb = prods[0:1, (T1 + T2) // P, :]

        out0 = pb("out0", [O, N])
        out1 = [pb(f"out1_{b}", [O, N]) for b in range(2)]
        acc3 = pb("acc3", [P, 2, BANK])
        tops = [acc3[:, 0, :], acc3[:, 1, :]]

        ids_in = sem("ids_in")
        rows_ready = sem("rows_ready")
        idx_ready = sem("idx_ready")
        gather_done = [sem(f"gather_done{g}") for g in range(2)]
        store_done = [sem(f"store_done{g}") for g in range(2)]
        w0_in = sem("w0_in")
        w1_in = sem("w1_in")
        wtop_in = sem("wtop_in")
        w0_summed = sem("w0_summed")
        w0_ready = sem("w0_ready")
        zeroed = sem("zeroed")
        x_loaded = [sem(f"x_loaded{b}") for b in range(2)]
        hid_loaded = [sem(f"hid_loaded{b}") for b in range(2)]
        prod_ready = sem("prod_ready")
        prod_used = sem("prod_used")
        half_ready = sem("half_ready")
        half_used = sem("half_used")
        act0_ready = sem("act0_ready")
        act1_ready = sem("act1_ready")
        pooled0_done = sem("pooled0_done")
        pooled1_done = sem("pooled1_done")
        top_ready = sem("top_ready")
        top_read = sem("top_read")
        y_ready = sem("y_ready")
        y_out = sem("y_out")

        X_DMAS = 1 + NT + 2
        HID_DMAS = 6

        block = ctx.enter_context(nc.Block())

        def wait(eng, s, value):
            if not isinstance(value, int) or value > 0:
                eng.wait_ge(s, value)

        @block.sync
        def _(sp):
            sp.dma_start(ids_sb[:, :], ids).then_inc(ids_in, 16)
            sp.dma_start(row_of_field[:, :], field_row).then_inc(ids_in, 16)
            for dst, src in ((w0_sb, w0_direct), (w0m_sb, w0_mirror)):
                sp.dma_start(dst[:, :, :], src).then_inc(w0_in, 16)
            for dst, src in ((w0h_sb, w0h_direct), (w0hm_sb, w0h_mirror), (half_sb, half_scale), (b0_sb, b0)):
                sp.dma_start(dst[:, :], src).then_inc(w0_in, 16)

            def store(k, g, nth):
                sp.wait_ge(gather_done[g], nth * 64)
                lower = xs[k, 0:F, :].rearrange("m (b c) -> (m b) c", c=4 * D)
                upper = xs[k, F:F + HALFTURN, :].rearrange("m (b c) -> (m b) c", c=4 * D)
                sp.dma_start(lower, gathered[g][:, :]).then_inc(store_done[g], 16)
                sp.dma_start(upper, gathered[g][0:HALFTURN * 4, :]).then_inc(store_done[g], 16)

            def load(k, b, nth):
                wait(sp, prod_ready, (k - 1) * US + U0)
                wait(sp, half_ready, k - 1)
                sp.wait_ge(store_done[b], nth * 32)
                tile = xs[k, 0:F, :]
                row = N
                for r in range(1):
                    src = bass.AP(tensor=tile.tensor, offset=tile.offset, ap=[[row, F], [0, R], [1, N]])
                    sp.dma_start(base[b][:, 0, :], src).then_inc(x_loaded[b], 16)
                for t in range(NT):
                    first = xs[k, R * t:F, :]
                    src = bass.AP(tensor=first.tensor, offset=first.offset, ap=[[row, F], [row, R], [1, N]])
                    sp.dma_start(rot[b][:, t, :], src).then_inc(x_loaded[b], 16)
                sp.dma_start(lo_half[b][:, :], xs[k, 0:HALFTURN, :]).then_inc(x_loaded[b], 16)
                sp.dma_start(hi_half[b][:, :], xs[k, HALFTURN:F, :]).then_inc(x_loaded[b], 16)

            store(0, 0, 1)
            load(0, 0, 1)
            sp.dma_start(w1_sb[:, :, :], w1).then_inc(w1_in, 16)
            sp.dma_start(b1_sb[:, :], b1).then_inc(w1_in, 16)
            store(1, 1, 1)
            load(1, 1, 1)
            sp.wait_ge(zeroed, 1)
            sp.dma_start(pooled0[0:CTX, :], dense).then_inc(wtop_in, 16)
            sp.dma_start(wt1a[0:CTX, :], wtop1[HID + O:HID + O + CTX, :]).then_inc(wtop_in, 16)
            sp.dma_start(wt1a[HID:P, :], wtop1[0:HID, :]).then_inc(wtop_in, 16)
            sp.dma_start(wt1b[:, :], wtop1[HID:HID + O, :]).then_inc(wtop_in, 16)
            sp.dma_start(bt1[:, :], btop1).then_inc(wtop_in, 16)
            sp.dma_start(wt2[:, :, :], wtop2).then_inc(wtop_in, 16)
            sp.dma_start(bt2[:, :], btop2).then_inc(wtop_in, 16)
            sp.dma_start(wt3[:, :], wtop3).then_inc(wtop_in, 16)
            store(2, 0, 2)
            with sp.Fori(1, NB // 2 - 1) as j:
                load(j * 2, 0, j + 1)
                store(j * 2 + 1, 1, j + 1)
                load(j * 2 + 1, 1, j + 1)
                store(j * 2 + 2, 0, j + 2)
            load(NB - 2, 0, NB // 2)
            store(NB - 1, 1, NB // 2)
            load(NB - 1, 1, NB // 2)

            sp.wait_ge(y_ready, 2)
            sp.dma_start(out, y_sb[:, :]).then_inc(y_out, 16)
            sp.wait_ge(y_out, 16)

        @block.gpsimd
        def _(pool):
            pool.wait_ge(ids_in, 32)
            nc.gpsimd.tensor_tensor(rows[:, :], ids_sb[:, :], row_of_field[:, 0:1].to_broadcast([P, NB * 4]),
                                    ALU.add).then_inc(rows_ready, 1)

            def pick(k, g):
                nc.gpsimd.tensor_copy(idx_now[g][:, :], rows[:, bass.ds(k * 4, 4)]).then_inc(idx_ready, 1)

            def gather(k, g, before, more=True):
                wait(pool, store_done[g], before * 32)
                if more:
                    wait(pool, gather_done[1 - g], (before + g) * 64)
                    pool.wait_ge(idx_ready, k + 1)
                    pick(k + 1, 1 - g)
                else:
                    pool.wait_ge(idx_ready, k + 1)
                for s in range(4):
                    nc.gpsimd.indirect_dma_start(
                        out=gathered[g][:, s * D:(s + 1) * D], out_offset=None, in_=table,
                        in_offset=bass.IndirectOffsetOnAxis(ap=idx_now[g][:, s:s + 1], axis=0),
                    ).then_inc(gather_done[g], 16)

            pool.wait_ge(rows_ready, 1)
            pick(0, 0)
            gather(0, 0, 0)
            gather(1, 1, 0)
            with pool.Fori(1, NB // 2 - 1) as j:
                gather(j * 2, 0, j)
                gather(j * 2 + 1, 1, j)
            gather(NB - 2, 0, NB // 2 - 1)
            gather(NB - 1, 1, NB // 2 - 1, more=False)

        @block.vector
        def _(dve):
            dve.wait_ge(w0_in, 16 * 6)
            nc.vector.tensor_tensor(w0_sb[:, :, :], w0_sb[:, :, :], w0m_sb[:, :, :], ALU.add).then_inc(w0_summed, 1)
            nc.vector.tensor_tensor(w0h_sb[:, :], w0h_sb[:, :], w0hm_sb[:, :], ALU.add).then_inc(w0_ready, 1)
            dve.wait_ge(w0_summed, 1)
            nc.vector.tensor_scalar(w0_sb[:, 0, :], w0_sb[:, 0, :], half_sb[:, 0:1], None,
                                    ALU.mult).then_inc(w0_ready, 1)
            nc.vector.memset(pooled0[:, :], 0.0)
            nc.vector.memset(wt1a[:, :], 0.0).then_inc(zeroed, 1)

            def unit(index, slot, factor, t):
                wait(dve, prod_used, index - RING + 1)
                nc.vector.tensor_tensor(prod[slot][:, :, :], t, factor.to_broadcast([P, UNIT, N]),
                                        ALU.mult).then_inc(prod_ready, 1)

            def layer0(k, b, nth, index, slot):
                dve.wait_ge(x_loaded[b], nth * X_DMAS * 16)
                wait(dve, half_used, k)
                nc.vector.tensor_tensor(prod_half[:, :], lo_half[b][:, :], hi_half[b][:, :],
                                        ALU.mult).then_inc(half_ready, 1)
                for u in range(U0):
                    unit(index + u, (slot + u) % RING, base[b][:, 0:1, :], rot[b][:, UNIT * u:UNIT * (u + 1), :])

            def layer1(b, first, last, index, slot):
                for u in range(first, last):
                    h, tu = u // (NT // UNIT), u % (NT // UNIT)
                    unit(index + u - first, (slot + u - first) % RING, hid[b][:, h:h + 1, :],
                         rot[b][:, UNIT * tu:UNIT * (tu + 1), :])

            def pool0(k, b):
                dve.wait_ge(act0_ready, k + 1)
                nc.vector.tensor_reduce(pooled0[HID:P, bass.ds(k * BS, BS)],
                                        act0[b][HID:P, :].rearrange("p (s d) -> p s d", d=D), axis=AX,
                                        op=ALU.add).then_inc(pooled0_done, 1)

            def pool1(k, b):
                dve.wait_ge(act1_ready, k + 1)
                nc.vector.tensor_reduce(pooled1[:, bass.ds(k * BS, BS)],
                                        act1[b][:, :].rearrange("p (s d) -> p s d", d=D), axis=AX,
                                        op=ALU.add).then_inc(pooled1_done, 1)

            def step(k, b, nth, more=True, back=True):
                index = k * US + U0
                dve.wait_ge(hid_loaded[b], nth * HID_DMAS * 16)
                layer1(b, 0, U1 // 2, index, U0 % RING)
                if back:
                    pool1(k - 1, 1 - b)
                pool0(k, b)
                if more:
                    layer0(k + 1, 1 - b, nth + b, index + U1 // 2, (U0 + U1 // 2) % RING)
                    layer1(b, U1 // 2, U1, index + U1 // 2 + U0, (U0 + U1 // 2 + U0) % RING)
                else:
                    layer1(b, U1 // 2, U1, index + U1 // 2, (U0 + U1 // 2) % RING)

            layer0(0, 0, 1, 0, 0)
            step(0, 0, 1, back=False)
            step(1, 1, 1)
            with dve.Fori(1, NB // 2 - 1) as j:
                step(j * 2, 0, j + 1)
                step(j * 2 + 1, 1, j + 1)
            step(NB - 2, 0, NB // 2)
            step(NB - 1, 1, NB // 2, more=False)
            pool1(NB - 1, 1)

        @block.tensor
        def _(pe):
            def unit(index, slot, acc, weights, first, last):
                pe.wait_ge(prod_ready, index + 1)
                for t in range(UNIT):
                    for h in range(HALVES):
                        mm = nc.tensor.matmul(acc[:, h * BANK:(h + 1) * BANK], weights[:, t, :],
                                              prod[slot][:, t, h * BANK:(h + 1) * BANK],
                                              start=first and t == 0, stop=last and t == UNIT - 1)
                mm.then_inc(prod_used, 1)

            def layer0(k, index, slot):
                pe.wait_ge(half_ready, k + 1)
                wait(pe, act0_ready, k)
                for h in range(HALVES):
                    mm = nc.tensor.matmul(out0[:, h * BANK:(h + 1) * BANK], w0h_sb[:, :],
                                          prod_half[:, h * BANK:(h + 1) * BANK], start=True, stop=False)
                mm.then_inc(half_used, 1)
                for u in range(U0):
                    unit(index + u, (slot + u) % RING, out0, w0_sb[:, UNIT * u:UNIT * (u + 1), :],
                              False, u == U0 - 1)

            def layer1(b, first, last, index, slot):
                for u in range(first, last):
                    unit(index + u - first, (slot + u - first) % RING, out1[b],
                              w1_sb[:, UNIT * u:UNIT * (u + 1), :], u == 0, u == U1 - 1)

            def step(k, b, more=True):
                index = k * US + U0
                wait(pe, act1_ready, k - 1)
                layer1(b, 0, U1 // 2, index, U0 % RING)
                if more:
                    layer0(k + 1, index + U1 // 2, (U0 + U1 // 2) % RING)
                    layer1(b, U1 // 2, U1, index + U1 // 2 + U0, (U0 + U1 // 2 + U0) % RING)
                else:
                    layer1(b, U1 // 2, U1, index + U1 // 2, (U0 + U1 // 2) % RING)

            pe.wait_ge(w0_ready, 2)
            layer0(0, 0, 0)
            pe.wait_ge(w1_in, 32)
            step(0, 0)
            step(1, 1)
            with pe.Fori(1, NB // 2 - 1) as j:
                step(j * 2, 0)
                step(j * 2 + 1, 1)
            step(NB - 2, 0)
            step(NB - 1, 1, more=False)

            pe.wait_ge(wtop_in, 16 * 8)
            pe.wait_ge(pooled0_done, NB)
            pe.wait_ge(pooled1_done, NB)
            n = 0

            def group(terms, rows_):
                nonlocal n
                if n >= 2:
                    pe.wait_ge(top_read, n - 1)
                for c, (w, x) in enumerate(terms):
                    mm = nc.tensor.matmul(tops[n % 2][0:rows_, :], w, x, start=c == 0, stop=c == len(terms) - 1)
                mm.then_inc(top_ready, 1)
                n += 1

            for s in range(2):
                cols = slice(s * BANK, (s + 1) * BANK)
                for m in range(T1 // P):
                    group([(wt1a[:, m * P:(m + 1) * P], pooled0[:, cols]),
                           (wt1b[:, m * P:(m + 1) * P], pooled1[:, cols])], P)
            for s in range(2):
                cols = slice(s * BANK, (s + 1) * BANK)
                pe.wait_ge(top_read, (s + 1) * (T1 // P))
                for m in range(T2 // P):
                    group([(wt2[:, c, m * P:(m + 1) * P], top1[:, c, cols]) for c in range(T1 // P)], P)
            for s in range(2):
                cols = slice(s * BANK, (s + 1) * BANK)
                pe.wait_ge(top_read, 2 * (T1 // P) + (s + 1) * (T2 // P))
                group([(wt3[:, c:c + 1], top2[:, c, cols]) for c in range(T2 // P)], 1)

        @block.scalar
        def _(act):
            def relu0(k, b, nth):
                act.wait_ge(prod_used, U0 if isinstance(k, int) and k == 0 else k * US - U1 // 2 + U0)
                wait(act, pooled0_done, k - 1)
                if not (isinstance(nth, int) and nth == 1):
                    act.wait_ge(hid_loaded[b], (nth - 1) * HID_DMAS * 16)
                nc.scalar.activation(act0[b][:, :], out0[:, :], ACT.Relu, bias=b0_sb[:, 0:1]).then_inc(act0_ready, 1)
                act.wait_ge(act0_ready, k + 1)
                wait(act, prod_ready, (k - 1) * US + U0)
                for h in range(NHT):
                    s, q = h // 2, h % 2
                    for dst, src, rows_ in (((0, 0, F),) if q == 0 else
                                            ((0, HALFTURN, HALFTURN), (HALFTURN, 0, HALFTURN))):
                        rows_sb = act0[b][F * s + src:F * s + src + rows_, :]
                        part = rows_sb.ap[0][0]
                        act.dma_start(
                            hid[b][R * dst:R * (dst + rows_), h, :],
                            bass.AP(tensor=rows_sb.tensor, offset=rows_sb.offset, ap=[[part, rows_], [0, R], [1, N]]),
                        ).then_inc(hid_loaded[b], 16)

            def relu1(k, b, last=False):
                act.wait_ge(prod_used, k * US + U0 + (U1 if last else US))
                wait(act, pooled1_done, k - 1)
                nc.scalar.activation(act1[b][:, :], out1[b][:, :], ACT.Relu, bias=b1_sb[:, 0:1]).then_inc(act1_ready, 1)

            act.wait_ge(w0_in, 16 * 6)
            relu0(0, 0, 1)
            act.wait_ge(w1_in, 32)
            relu0(1, 1, 1)
            relu1(0, 0)
            relu0(2, 0, 2)
            relu1(1, 1)
            with act.Fori(1, NB // 2 - 1) as j:
                relu0(j * 2 + 1, 1, j + 1)
                relu1(j * 2, 0)
                relu0(j * 2 + 2, 0, j + 2)
                relu1(j * 2 + 1, 1)
            relu0(NB - 1, 1, NB // 2)
            relu1(NB - 2, 0)
            relu1(NB - 1, 1, last=True)

            act.wait_ge(wtop_in, 16 * 8)
            n = 0
            for layer, dst, bias, tiles in ((1, top1, bt1, T1 // P), (2, top2, bt2, T2 // P)):
                for s in range(2):
                    for m in range(tiles):
                        act.wait_ge(top_ready, n + 1)
                        nc.scalar.activation(dst[:, m, s * BANK:(s + 1) * BANK], tops[n % 2], ACT.Relu,
                                             bias=bias[:, m:m + 1]).then_inc(top_read, 1)
                        n += 1
            for s in range(2):
                act.wait_ge(top_ready, n + 1)
                nc.scalar.copy(y_sb[0:1, s * BANK:(s + 1) * BANK], tops[n % 2][0:1, :]).then_inc(y_ready, 1)
                n += 1


def kernel(**inputs):
    import numpy as np
    import concourse.bacc as bacc
    from concourse.bass_utils import run_bass_kernel_spmd

    f32 = np.dtype("float32")
    i32 = np.dtype("int32")
    a = {name: np.asarray(value) for name, value in inputs.items()}

    p = np.arange(P)
    i, r = p // R, p % R
    starts = np.concatenate([[0], np.cumsum(VOCABS)[:-1]]).astype(i32)
    field_row = starts[i].reshape(P, 1)
    half_scale = np.where(r == 0, 0.5, 1.0).astype(f32).reshape(P, 1)
    t = np.arange(NT)
    field = (i[:, None] + R * t[None, :] + r[:, None]) % F
    first = np.repeat(i[:, None], NT, axis=1)
    hq = np.arange(NHT)
    hidden = F * (hq // 2)[None, :] + (i[:, None] + HALFTURN * (hq % 2)[None, :]) % F
    chunk = hidden[:, :, None] * F + field[:, None, :]
    ih = np.arange(HALFTURN)

    ids = a["ids"].reshape(NB, 4, 4, F).transpose(3, 1, 0, 2).reshape(P, NB * 4)
    W0T = a["L0_rec_W0"].T
    W1T = a["L0_rec_W1"].T
    arrays = {
        "table": np.concatenate([a[f"tbl_{f}"] for f in range(F)], axis=0),
        "ids": ids,
        "field_row": field_row,
        "half_scale": half_scale,
        "w0_direct": W0T[first * F + field],
        "w0_mirror": W0T[field * F + first],
        "w0h_direct": W0T[ih * F + ih + HALFTURN],
        "w0h_mirror": W0T[(ih + HALFTURN) * F + ih],
        "w1": W1T[chunk].reshape(P, NHT * NT, O),
        "b0": a["L0_rec_b0"].reshape(O, 1),
        "b1": a["L0_rec_b1"].reshape(O, 1),
        "dense": a["dense_ctx"].T,
        "wtop1": a["W_top1"],
        "btop1": a["b_top1"].reshape(T1 // P, P).T,
        "wtop2": a["W_top2"].reshape(T1 // P, P, T2).transpose(1, 0, 2),
        "btop2": a["b_top2"].reshape(T2 // P, P).T,
        "wtop3": a["W_top3"].reshape(T2 // P, P).T,
    }
    arrays = {name: np.ascontiguousarray(v) for name, v in arrays.items()}

    nc = bacc.Bacc("TRN2", target_bir_lowering=False, num_devices=1)
    aps = {name: nc.dram_tensor(name, v.shape, mybir.dt.from_np(v.dtype), kind="ExternalInput").ap()
           for name, v in arrays.items()}
    y = nc.dram_tensor("y", (1, B), mybir.dt.from_np(f32), kind="ExternalOutput").ap()
    build_tower(nc, out=y, **aps)
    res = run_bass_kernel_spmd(nc, [arrays], core_ids=[0])
    return res.results[0]["y"].reshape(B, 1)
```

```python
import concourse.bass as bass
from concourse import mybir
from contextlib import ExitStack

VOCABS = [12500, 125000, 1250, 125000, 1000, 12500, 1000, 125000, 1000, 12500, 1250, 1250, 1250, 1000, 12500, 1000,
          1000, 12500, 1000, 1250, 1000, 1250, 1250, 1250, 1000, 1000, 1000, 1250, 12500, 1000, 1250, 1250]
P = 128
B = 1024
F = 32
D = 64
O = 128
HID = 64
CTX = 16
T1 = 512
T2 = 256

BS = 16
N = BS * D
NB = B // BS
BANK = 512
HALVES = N // BANK

R = 4
NT = 4
NHT = 4
UNIT = 2
RING = 5
U0 = NT // UNIT
U1 = NHT * NT // UNIT
US = U0 + U1
HALFTURN = F // 2
CG = P // HALFTURN
CN = N // CG

L1_HEAD = 2
FULL_STEP = [(1, n) for n in range(L1_HEAD)] + [(0, n) for n in range(U0)] + [(1, n) for n in range(L1_HEAD, U1)]
LAST_STEP = [(1, n) for n in range(U1)]
FIRST_UNITS = [(0, n) for n in range(U0)]
ROT01_DONE = 6
OUT0_DONE = L1_HEAD + U0

WHOLE = {(0, 1), (1, 4)}
SPLIT = [x for x in FIRST_UNITS + LAST_STEP if x not in WHOLE]
SPLITS_FIRST = sum(x in SPLIT for x in FIRST_UNITS)
SPLITS_STEP = len(SPLIT)
LAG = 1


def splits_before(k, step, pos):
    return k * SPLITS_STEP + SPLITS_FIRST + sum(x in SPLIT for x in step[:pos])


def build_tower(nc, table, ids, field_row, half_scale, w0_direct, w0_mirror, w0h_direct, w0h_mirror, w1,
                b0, b1, dense, wtop1, btop1, wtop2, btop2, wtop3, out):
    fp32 = mybir.dt.float32
    i32 = mybir.dt.int32
    f32r = mybir.dt.float32r
    ALU = mybir.AluOpType
    ACT = mybir.ActivationFunctionType

    ctx = ExitStack()
    with ctx:
        def sb(name, shape, dt=fp32):
            return ctx.enter_context(nc.sbuf_tensor(name, shape, dt))

        def pb(name, shape):
            return ctx.enter_context(nc.psum_tensor(name, shape, fp32))

        def sem(name):
            return ctx.enter_context(nc.semaphore(name))

        xs = nc.dram_tensor("xs", [NB, F + HALFTURN, N], fp32).ap()

        ids_sb = sb("ids_sb", [P, NB * 4], i32)
        row_of_field = sb("row_of_field", [P, 1], i32)
        rows = sb("rows", [P, NB * 4], i32)
        idx_now = [sb(f"idx_now{g}", [P, 4], i32) for g in range(2)]
        gathered = [sb(f"gathered{g}", [P, 4 * D]) for g in range(2)]
        base = [sb(f"base{b}", [P, 1, N]) for b in range(2)]
        rot = [sb(f"rot{b}", [P, NT, N]) for b in range(2)]
        hid = [sb(f"hid{b}", [P, NHT, N]) for b in range(2)]
        prods = sb("prods", [P, RING * UNIT, N])
        prod = [prods[:, u * UNIT:(u + 1) * UNIT, :] for u in range(RING)]
        prod_hi = [sb(f"prod_hi{u}", [P, N], f32r) for u in range(RING)]
        prod_lo = [sb(f"prod_lo{u}", [P, N], f32r) for u in range(RING)]
        turn_a = [sb(f"turn_a{b}", [P, CN]) for b in range(2)]
        turn_b = [sb(f"turn_b{b}", [P, CN]) for b in range(2)]
        turn = sb("turn", [P, CN])
        turn_hi = [sb(f"turn_hi{b}", [P, CN], f32r) for b in range(2)]
        turn_lo = [sb(f"turn_lo{b}", [P, CN], f32r) for b in range(2)]
        stack = [sb(f"stack{b}", [4 * HALFTURN, N], f32r) for b in range(2)]
        act0 = [sb(f"act0_{b}", [HID, N]) for b in range(2)]
        sums0 = sb("sums0", [P, BS])
        sums1 = sb("sums1", [P, BS])
        w0_sb = sb("w0_sb", [P, NT, O])
        half_sb = sb("half_sb", [P, 1])
        w1_sb = sb("w1_sb", [P, NHT * NT, O])
        w_hi = {x: sb(f"w_hi{x[0]}_{x[1]}", [P, O], f32r) for x in SPLIT}
        w_lo = {x: sb(f"w_lo{x[0]}_{x[1]}", [P, O], f32r) for x in SPLIT}
        w_turn = sb("w_turn", [4 * HALFTURN, O])
        w_turn_m = sb("w_turn_m", [4 * HALFTURN, O])
        w_stack = sb("w_stack", [4 * HALFTURN, O], f32r)
        w_turn_hi = sb("w_turn_hi", [4 * HALFTURN, O], f32r)
        b0_sb = sb("b0_sb", [O, 1])
        b1_sb = sb("b1_sb", [O, 1])
        w0m_sb = prods[:, 0, 0:NT * O].rearrange("p (t o) -> p t o", t=NT)
        pooled0 = sb("pooled0", [P, B])
        pooled1 = sb("pooled1", [P, B])
        wt1a = hid[0][:, 0, 0:T1]
        wt1b = hid[0][:, 0, T1:2 * T1]
        bt1 = sb("bt1", [P, T1 // P])
        wt2 = hid[0][:, 1, :].rearrange("p (c n) -> p c n", n=T2)
        bt2 = sb("bt2", [P, T2 // P])
        wt3 = sb("wt3", [P, T2 // P])
        top1 = prods[:, 0:T1 // P, :]
        top2 = prods[:, T1 // P:(T1 + T2) // P, :]
        y_sb = prods[0:1, (T1 + T2) // P, :]

        out0 = pb("out0", [O, N])
        out1 = [pb(f"out1_{b}", [O, N]) for b in range(2)]
        acc3 = pb("acc3", [P, 2, BANK])
        tops = [acc3[:, 0, :], acc3[:, 1, :]]

        ids_in = sem("ids_in")
        rows_ready = sem("rows_ready")
        idx_ready = sem("idx_ready")
        gather_done = [sem(f"gather_done{g}") for g in range(2)]
        store_done = [sem(f"store_done{g}") for g in range(2)]
        w0_in = sem("w0_in")
        w1_in = sem("w1_in")
        wtop_in = sem("wtop_in")
        w0_summed = sem("w0_summed")
        w0_whole = sem("w0_whole")
        w0_ready = sem("w0_ready")
        w1_ready = sem("w1_ready")
        w0_hi_ready = sem("w0_hi_ready")
        w1_hi_ready = sem("w1_hi_ready")
        zeroed = sem("zeroed")
        x_loaded = [sem(f"x_loaded{b}") for b in range(2)]
        turn_loaded = [sem(f"turn_loaded{b}") for b in range(2)]
        turn_made = sem("turn_made")
        turn_hi_ready = sem("turn_hi_ready")
        turn_lo_ready = sem("turn_lo_ready")
        stack_loaded = [sem(f"stack_loaded{b}") for b in range(2)]
        stack_used = sem("stack_used")
        hid_loaded = [[sem(f"hid_loaded{b}_{h}") for h in range(NHT)] for b in range(2)]
        prod_ready = sem("prod_ready")
        hi_ready = sem("hi_ready")
        lo_ready = sem("lo_ready")
        prod_used = sem("prod_used")
        act0_ready = sem("act0_ready")
        sums0_ready = sem("sums0_ready")
        sums1_ready = sem("sums1_ready")
        pooled0_done = sem("pooled0_done")
        pooled1_done = sem("pooled1_done")
        top_ready = sem("top_ready")
        top_read = sem("top_read")
        y_ready = sem("y_ready")
        y_out = sem("y_out")

        X_DMAS = 1 + NT
        HID_DMAS = [1, 2, 1, 2]

        block = ctx.enter_context(nc.Block())

        def at(k, ph, j, ahead):
            return k + ahead, (ph + ahead) % 2, j + (ph + ahead) // 2 + 1

        def steps(eng, step):
            for k in range(2):
                step(k, k, 0)
            with eng.Fori(1, NB // 2 - 2) as j:
                step(j * 2, 0, j)
                step(j * 2 + 1, 1, j)
            for k in range(NB - 4, NB):
                step(k, k % 2, k // 2)

        def wait(eng, s, value):
            if not isinstance(value, int) or value > 0:
                eng.wait_ge(s, value)

        def work_out(eng, *values):
            for value in values:
                if not isinstance(value, int):
                    eng.compute_val(value)

        @block.sync
        def _(sp):
            sp.dma_start(ids_sb[:, :], ids).then_inc(ids_in, 16)
            sp.dma_start(row_of_field[:, :], field_row).then_inc(ids_in, 16)
            def store(k, g, nth):
                sp.wait_ge(gather_done[g], nth * 64)
                lower = xs[k, 0:F, :].rearrange("m (b c) -> (m b) c", c=4 * D)
                upper = xs[k, F:F + HALFTURN, :].rearrange("m (b c) -> (m b) c", c=4 * D)
                sp.dma_start(lower, gathered[g][:, :]).then_inc(store_done[g], 16)
                sp.dma_start(upper, gathered[g][0:HALFTURN * 4, :]).then_inc(store_done[g], 16)

            def load_turn(k, b, nth):
                work_out(sp, nth * 32, k - 1)
                sp.wait_ge(store_done[b], nth * 32)
                wait(sp, turn_made, k - 1)
                sp.dma_start(turn_a[b][:, :],
                             xs[k, 0:HALFTURN, :].rearrange("m (c n) -> (m c) n", n=CN)).then_inc(turn_loaded[b], 16)
                sp.dma_start(turn_b[b][:, :],
                             xs[k, HALFTURN:F, :].rearrange("m (c n) -> (m c) n", n=CN)).then_inc(turn_loaded[b], 16)

            def load_rot(k, b, t):
                first = xs[k, R * t:F, :]
                src = bass.AP(tensor=first.tensor, offset=first.offset, ap=[[N, F], [N, R], [1, N]])
                sp.dma_start(rot[b][:, t, :], src).then_inc(x_loaded[b], 16)

            def load_head(k, b, nth):
                work_out(sp, (k - 2) * US + U0 + ROT01_DONE, nth * 32)
                wait(sp, prod_ready, (k - 2) * US + U0 + ROT01_DONE)
                sp.wait_ge(store_done[b], nth * 32)
                first = xs[k, 0:F, :]
                src = bass.AP(tensor=first.tensor, offset=first.offset, ap=[[N, F], [0, R], [1, N]])
                sp.dma_start(base[b][:, 0, :], src).then_inc(x_loaded[b], 16)
                load_rot(k, b, 0)
                load_rot(k, b, 1)

            def load_tail(k, b):
                wait(sp, prod_ready, (k - 1) * US + U0)
                load_rot(k, b, 2)
                load_rot(k, b, 3)

            def copy_stack(k, b):
                work_out(sp, k + 1, k - 1)
                sp.wait_ge(turn_lo_ready, k + 1)
                wait(sp, stack_used, k - 1)
                for g in range(4):
                    rows_of_part = stack[b][g * HALFTURN:(g + 1) * HALFTURN, :].bitcast(fp32)
                    sp.dma_start(rows_of_part.rearrange("m (c n) -> m c n", n=CN),
                                 (turn_hi, turn_lo)[g % 2][b][:, :].bitcast(fp32)).then_inc(stack_loaded[b], 16)

            store(0, 0, 1)
            load_turn(0, 0, 1)
            load_head(0, 0, 1)
            load_tail(0, 0)
            for dst, src in ((w0_sb[:, :, :], w0_direct), (w0m_sb, w0_mirror), (w_turn[:, :], w0h_direct),
                             (w_turn_m[:, :], w0h_mirror), (half_sb[:, :], half_scale), (b0_sb[:, :], b0)):
                sp.dma_start(dst, src).then_inc(w0_in, 16)
            copy_stack(0, 0)
            store(1, 1, 1)
            load_turn(1, 1, 1)
            sp.dma_start(w1_sb[:, :, :], w1).then_inc(w1_in, 16)
            sp.dma_start(b1_sb[:, :], b1).then_inc(w1_in, 16)
            load_head(1, 1, 1)
            load_tail(1, 1)
            store(2, 0, 2)
            load_turn(2, 0, 2)
            copy_stack(1, 1)
            sp.wait_ge(zeroed, 1)
            sp.dma_start(pooled0[0:CTX, :], dense).then_inc(wtop_in, 16)
            sp.dma_start(bt1[:, :], btop1).then_inc(wtop_in, 16)
            sp.dma_start(bt2[:, :], btop2).then_inc(wtop_in, 16)
            sp.dma_start(wt3[:, :], wtop3).then_inc(wtop_in, 16)

            def step(k, ph, j):
                last = k if isinstance(k, int) else 0
                if last + 3 < NB:
                    store(*at(k, ph, j, 3))
                    load_turn(*at(k, ph, j, 3))
                if last + 2 < NB:
                    load_head(*at(k, ph, j, 2))
                    copy_stack(*at(k, ph, j, 2)[:2])
                    load_tail(*at(k, ph, j, 2)[:2])

            steps(sp, step)

            sp.wait_ge(zeroed, 2)
            sp.dma_start(wt1a[0:CTX, :], wtop1[HID + O:HID + O + CTX, :]).then_inc(wtop_in, 16)
            sp.dma_start(wt1a[HID:P, :], wtop1[0:HID, :]).then_inc(wtop_in, 16)
            sp.dma_start(wt1b, wtop1[HID:HID + O, :]).then_inc(wtop_in, 16)
            sp.dma_start(wt2, wtop2).then_inc(wtop_in, 16)
            sp.wait_ge(y_ready, 2)
            sp.dma_start(out, y_sb[:, :]).then_inc(y_out, 16)
            sp.wait_ge(y_out, 16)

        @block.gpsimd
        def _(pool):
            pool.wait_ge(ids_in, 32)
            nc.gpsimd.tensor_tensor(rows[:, :], ids_sb[:, :], row_of_field[:, 0:1].to_broadcast([P, NB * 4]),
                                    ALU.add).then_inc(rows_ready, 1)

            def pick(k, g):
                nc.gpsimd.tensor_copy(idx_now[g][:, :], rows[:, bass.ds(k * 4, 4)]).then_inc(idx_ready, 1)

            def gather(k, g, before, more=True):
                wait(pool, store_done[g], before * 32)
                if more:
                    wait(pool, gather_done[1 - g], (before + g) * 64)
                    pool.wait_ge(idx_ready, k + 1)
                    pick(k + 1, 1 - g)
                else:
                    pool.wait_ge(idx_ready, k + 1)
                for s in range(4):
                    nc.gpsimd.indirect_dma_start(
                        out=gathered[g][:, s * D:(s + 1) * D], out_offset=None, in_=table,
                        in_offset=bass.IndirectOffsetOnAxis(ap=idx_now[g][:, s:s + 1], axis=0),
                    ).then_inc(gather_done[g], 16)

            pool.wait_ge(rows_ready, 1)
            pick(0, 0)
            gather(0, 0, 0)
            gather(1, 1, 0)
            with pool.Fori(1, NB // 2 - 1) as j:
                gather(j * 2, 0, j)
                gather(j * 2 + 1, 1, j)
            gather(NB - 2, 0, NB // 2 - 1)
            gather(NB - 1, 1, NB // 2 - 1, more=False)

        @block.vector
        def _(dve):
            nc.vector.memset(pooled0[:, :], 0.0).then_inc(zeroed, 1)

            def make_turn(k, b, nth):
                dve.wait_ge(turn_loaded[b], nth * 32)
                wait(dve, turn_lo_ready, k)
                nc.vector.tensor_tensor(turn[:, :], turn_a[b][:, :], turn_b[b][:, :], ALU.mult).then_inc(turn_made, 1)
                if not (isinstance(nth, int) and nth == 1):
                    dve.wait_ge(stack_loaded[b], (nth - 1) * 64)
                dve.wait_ge(turn_made, k + 1)
                nc.vector.tensor_copy(turn_hi[b][:, :], turn[:, :]).then_inc(turn_hi_ready, 1)
                dve.wait_ge(turn_hi_ready, k + 1)
                nc.vector.tensor_tensor(turn_lo[b][:, :], turn[:, :], turn_hi[b][:, :].bitcast(fp32),
                                        ALU.subtract).then_inc(turn_lo_ready, 1)

            def product(index, slot, factor, tiles):
                wait(dve, prod_used, index - RING + 1)
                nc.vector.tensor_tensor(prod[slot][:, :, :], tiles, factor.to_broadcast([P, UNIT, N]),
                                        ALU.mult).then_inc(prod_ready, 1)

            def low_part(slot, nth):
                dve.wait_ge(hi_ready, nth)
                nc.vector.tensor_tensor(prod_lo[slot][:, :], prod[slot][:, 0, :], prod_hi[slot][:, :].bitcast(fp32),
                                        ALU.subtract).then_inc(lo_ready, 1)

            def low_parts(k, order, first, last):
                for pos in range(first, last):
                    if order[pos] in SPLIT:
                        low_part((U0 + pos) % RING, splits_before(k, order, pos) + 1)

            make_turn(0, 0, 1)
            dve.wait_ge(w0_in, 16 * 6)
            nc.vector.tensor_tensor(w0_sb[:, :, :], w0_sb[:, :, :], w0m_sb, ALU.add).then_inc(w0_summed, 1)
            nc.vector.tensor_tensor(w_turn[:, :], w_turn[:, :], w_turn_m[:, :], ALU.add).then_inc(w0_summed, 1)
            dve.wait_ge(w0_summed, 2)
            nc.vector.tensor_scalar(w0_sb[:, 0, :], w0_sb[:, 0, :], half_sb[:, 0:1], None,
                                    ALU.mult).then_inc(w0_whole, 1)
            half = 2 * HALFTURN
            nc.vector.tensor_copy(w_turn_hi[:, :], w_turn[:, :]).then_inc(w0_whole, 1)
            nc.vector.tensor_copy(w_stack[0:half, :], w_turn[0:half, :]).then_inc(w0_ready, 1)
            dve.wait_ge(w0_whole, 2)
            nc.vector.tensor_tensor(w_stack[half:2 * half, :], w_turn[half:2 * half, :],
                                    w_turn_hi[half:2 * half, :].bitcast(fp32), ALU.subtract).then_inc(w0_ready, 1)
            dve.wait_ge(x_loaded[0], X_DMAS * 16)
            for n in range(U0):
                product(n, n, base[0][:, 0:1, :], rot[0][:, UNIT * n:UNIT * (n + 1), :])
            dve.wait_ge(w0_hi_ready, SPLITS_FIRST)
            for x in SPLIT:
                if x[0] == 0:
                    nc.vector.tensor_tensor(w_lo[x][:, :], w0_sb[:, UNIT * x[1], :], w_hi[x][:, :].bitcast(fp32),
                                            ALU.subtract).then_inc(w0_ready, 1)
            done = 0
            for n in range(U0):
                if (0, n) in SPLIT:
                    done += 1
                    low_part(n, done)
            make_turn(1, 1, 1)
            dve.wait_ge(w1_hi_ready, SPLITS_STEP - SPLITS_FIRST)
            for x in SPLIT:
                if x[0] == 1:
                    nc.vector.tensor_tensor(w_lo[x][:, :], w1_sb[:, UNIT * x[1], :], w_hi[x][:, :].bitcast(fp32),
                                            ALU.subtract).then_inc(w1_ready, 1)

            def step(k, ph, j):
                number = k if isinstance(k, int) else 0
                order = FULL_STEP if number < NB - 1 else LAST_STEP
                _, b, nth = at(k, ph, j, 0)
                _, nb, nnth = at(k, ph, j, 1)
                if order is LAST_STEP:
                    dve.wait_ge(prod_ready, k * US + U0)
                    nc.vector.memset(wt1a, 0.0).then_inc(zeroed, 1)
                for pos, (layer, n) in enumerate(order):
                    index, slot = k * US + U0 + pos, (U0 + pos) % RING
                    if layer == 1:
                        h, tiles = n % NHT, UNIT * (n // NHT)
                        if n < NHT:
                            dve.wait_ge(hid_loaded[b][h], nth * HID_DMAS[h] * 16)
                        product(index, slot, hid[b][:, h:h + 1, :], rot[b][:, tiles:tiles + UNIT, :])
                    else:
                        if n == 0:
                            dve.wait_ge(x_loaded[nb], nnth * X_DMAS * 16)
                        product(index, slot, base[nb][:, 0:1, :], rot[nb][:, UNIT * n:UNIT * (n + 1), :])
                    if pos >= LAG:
                        low_parts(k, order, pos - LAG, pos - LAG + 1)
                    elif not (number == 0 and isinstance(k, int)):
                        low_parts(k - 1, FULL_STEP, US - LAG + pos, US - LAG + pos + 1)
                    if pos == ROT01_DONE - 1 and number + 2 < NB:
                        make_turn(*at(k, ph, j, 2))
                if order is LAST_STEP:
                    low_parts(k, order, len(order) - LAG, len(order))

            steps(dve, step)

        @block.tensor
        def _(pe):
            def unit(index, slot, acc, x, weights, nth, first, last):
                pe.wait_ge(prod_ready, index + 1)
                cols = [slice(h * BANK, (h + 1) * BANK) for h in range(HALVES)]
                whole = [1, 0] if x in WHOLE else [1]
                for t in whole:
                    for c in cols:
                        mm = nc.tensor.matmul(acc[:, c], weights[:, t, :], prod[slot][:, t, c],
                                              start=first and t == 1, stop=last and t == whole[-1] and x in WHOLE)
                if x in SPLIT:
                    pe.wait_ge(lo_ready, nth)
                    for w, z in ((w_hi[x], prod_hi[slot]), (w_hi[x], prod_lo[slot]), (w_lo[x], prod_hi[slot])):
                        for c in cols:
                            mm = nc.tensor.matmul(acc[:, c], w[:, :], z[:, c], start=False,
                                                  stop=last and w is w_lo[x])
                mm.then_inc(prod_used, 1)

            def turn_pairs(k, b, nth):
                pe.wait_ge(stack_loaded[b], nth * 64)
                wait(pe, sums0_ready, k)
                for h in range(HALVES):
                    mm = nc.tensor.matmul(out0[:, h * BANK:(h + 1) * BANK], w_stack[:, :],
                                          stack[b][:, h * BANK:(h + 1) * BANK], start=True, stop=False)
                mm.then_inc(stack_used, 1)

            def layer0_unit(index, slot, n, nth):
                unit(index, slot, out0, (0, n), w0_sb[:, UNIT * n:UNIT * (n + 1), :], nth, False, n == U0 - 1)

            pe.wait_ge(w0_ready, 2 + SPLITS_FIRST)
            turn_pairs(0, 0, 1)
            for n in range(U0):
                layer0_unit(n, n, n, sum((0, m) in SPLIT for m in range(n + 1)))
            pe.wait_ge(w1_in, 32)
            pe.wait_ge(w1_ready, SPLITS_STEP - SPLITS_FIRST)

            def step(k, ph, j):
                number = k if isinstance(k, int) else 0
                order = FULL_STEP if number < NB - 1 else LAST_STEP
                _, b, _ = at(k, ph, j, 0)
                wait(pe, sums1_ready, k - 1)
                for pos, (layer, n) in enumerate(order):
                    index, slot = k * US + U0 + pos, (U0 + pos) % RING
                    nth = splits_before(k, order, pos) + 1
                    if layer == 0:
                        if n == 0:
                            turn_pairs(*at(k, ph, j, 1))
                        layer0_unit(index, slot, n, nth)
                    else:
                        unit(index, slot, out1[b], (1, n), w1_sb[:, UNIT * n:UNIT * (n + 1), :], nth,
                             n == 0, n == U1 - 1)

            steps(pe, step)

            pe.wait_ge(wtop_in, 16 * 8)
            pe.wait_ge(pooled0_done, NB)
            pe.wait_ge(pooled1_done, NB)
            n = 0

            def group(terms, rows_):
                nonlocal n
                if n >= 2:
                    pe.wait_ge(top_read, n - 1)
                for c, (w, x) in enumerate(terms):
                    mm = nc.tensor.matmul(tops[n % 2][0:rows_, :], w, x, start=c == 0, stop=c == len(terms) - 1)
                mm.then_inc(top_ready, 1)
                n += 1

            for s in range(2):
                cols = slice(s * BANK, (s + 1) * BANK)
                for m in range(T1 // P):
                    group([(wt1a[:, m * P:(m + 1) * P], pooled0[:, cols]),
                           (wt1b[:, m * P:(m + 1) * P], pooled1[:, cols])], P)
            for s in range(2):
                cols = slice(s * BANK, (s + 1) * BANK)
                pe.wait_ge(top_read, (s + 1) * (T1 // P))
                for m in range(T2 // P):
                    group([(wt2[:, c, m * P:(m + 1) * P], top1[:, c, cols]) for c in range(T1 // P)], P)
            for s in range(2):
                cols = slice(s * BANK, (s + 1) * BANK)
                pe.wait_ge(top_read, 2 * (T1 // P) + (s + 1) * (T2 // P))
                group([(wt3[:, c:c + 1], top2[:, c, cols]) for c in range(T2 // P)], 1)

        @block.scalar
        def _(act):
            def high_part(index, slot):
                act.wait_ge(prod_ready, index + 1)
                nc.scalar.copy(prod_hi[slot][:, :], prod[slot][:, 0, :]).then_inc(hi_ready, 1)

            def relu0(k, b, nth, summed):
                act.wait_ge(prod_used, summed)
                if not (isinstance(nth, int) and nth == 1):
                    for h in range(NHT):
                        act.wait_ge(hid_loaded[b][h], (nth - 1) * HID_DMAS[h] * 16)
                nc.scalar.activation(act0[b][0:HID, :], out0[0:HID, :], ACT.Relu,
                                     bias=b0_sb[0:HID, 0:1]).then_inc(act0_ready, 1)
                act.wait_ge(act0_ready, k + 1)
                wait(act, prod_ready, (k - 1) * US + U0)
                for h in range(NHT):
                    s, q = h // 2, h % 2
                    for dst, src, rows_ in (((0, 0, F),) if q == 0 else
                                            ((0, HALFTURN, HALFTURN), (HALFTURN, 0, HALFTURN))):
                        rows_sb = act0[b][F * s + src:F * s + src + rows_, :]
                        part = rows_sb.ap[0][0]
                        act.dma_start(
                            hid[b][R * dst:R * (dst + rows_), h, :],
                            bass.AP(tensor=rows_sb.tensor, offset=rows_sb.offset, ap=[[part, rows_], [0, R], [1, N]]),
                        ).then_inc(hid_loaded[b][h], 16)

            def pool0(k, b, first, last):
                if first == 0:
                    wait(act, pooled0_done, k)
                for s in range(first, last):
                    c = slice(s * D, (s + 1) * D)
                    a = nc.scalar.activation(out0[HID:P, c], out0[HID:P, c], ACT.Relu, bias=b0_sb[HID:P, 0:1],
                                             accum_out=sums0[HID:P, s:s + 1])
                if last == BS:
                    a.then_inc(sums0_ready, 1)
                    act.wait_ge(sums0_ready, k + 1)
                    nc.scalar.copy(pooled0[HID:P, bass.ds(k * BS, BS)], sums0[HID:P, :]).then_inc(pooled0_done, 1)

            def pool1(k, b, first, last, summed=None):
                if first == 0:
                    act.wait_ge(prod_used, summed)
                    wait(act, pooled1_done, k)
                for s in range(first, last):
                    c = slice(s * D, (s + 1) * D)
                    a = nc.scalar.activation(out1[b][:, c], out1[b][:, c], ACT.Relu, bias=b1_sb[:, 0:1],
                                             accum_out=sums1[:, s:s + 1])
                if last == BS:
                    a.then_inc(sums1_ready, 1)
                    act.wait_ge(sums1_ready, k + 1)
                    nc.scalar.copy(pooled1[:, bass.ds(k * BS, BS)], sums1[:, :]).then_inc(pooled1_done, 1)

            act.wait_ge(w0_whole, 2)
            for x in SPLIT:
                if x[0] == 0:
                    nc.scalar.copy(w_hi[x][:, :], w0_sb[:, UNIT * x[1], :]).then_inc(w0_hi_ready, 1)
            for n in range(U0):
                if (0, n) in SPLIT:
                    high_part(n, n)
            act.wait_ge(w1_in, 32)
            for x in SPLIT:
                if x[0] == 1:
                    nc.scalar.copy(w_hi[x][:, :], w1_sb[:, UNIT * x[1], :]).then_inc(w1_hi_ready, 1)
            relu0(0, 0, 1, U0)
            pool0(0, 0, 0, BS - 4)

            POOL1_AT = {3: (0, 5), 4: (5, 10), 5: (10, 16)}
            RELU0_AT = 6
            POOL0_AT = {7: (0, 4), 8: (4, 8), 9: (8, 12)}

            def step(k, ph, j):
                number = k if isinstance(k, int) else 0
                first = isinstance(k, int) and k == 0
                order = FULL_STEP if number < NB - 1 else LAST_STEP
                _, b, _ = at(k, ph, j, 0)
                nk, nb, nnth = at(k, ph, j, 1)
                for pos, x in enumerate(order):
                    if x in SPLIT:
                        high_part(k * US + U0 + pos, (U0 + pos) % RING)
                    if pos == 0:
                        pool0(k, b, BS - 4, BS)
                    if pos in POOL1_AT and not first:
                        pool1(k - 1, nb, *POOL1_AT[pos], k * US + U0)
                    if pos == RELU0_AT and order is FULL_STEP:
                        relu0(nk, nb, nnth, k * US + U0 + OUT0_DONE)
                    if pos in POOL0_AT and order is FULL_STEP:
                        pool0(nk, nb, *POOL0_AT[pos])

            steps(act, step)
            pool1(NB - 1, (NB - 1) % 2, 0, BS, (NB - 1) * US + U0 + len(LAST_STEP))

            act.wait_ge(wtop_in, 16 * 8)
            n = 0
            for layer, dst, bias, tiles in ((1, top1, bt1, T1 // P), (2, top2, bt2, T2 // P)):
                for s in range(2):
                    for m in range(tiles):
                        act.wait_ge(top_ready, n + 1)
                        nc.scalar.activation(dst[:, m, s * BANK:(s + 1) * BANK], tops[n % 2], ACT.Relu,
                                             bias=bias[:, m:m + 1]).then_inc(top_read, 1)
                        n += 1
            for s in range(2):
                act.wait_ge(top_ready, n + 1)
                nc.scalar.copy(y_sb[0:1, s * BANK:(s + 1) * BANK], tops[n % 2][0:1, :]).then_inc(y_ready, 1)
                n += 1


def kernel(**inputs):
    import numpy as np
    import concourse.bacc as bacc
    from concourse.bass_utils import run_bass_kernel_spmd

    f32 = np.dtype("float32")
    i32 = np.dtype("int32")
    a = {name: np.asarray(value) for name, value in inputs.items()}

    p = np.arange(P)
    i, r = p // R, p % R
    starts = np.concatenate([[0], np.cumsum(VOCABS)[:-1]]).astype(i32)
    field_row = starts[i].reshape(P, 1)
    half_scale = np.where(r == 0, 0.5, 1.0).astype(f32).reshape(P, 1)
    t = np.arange(NT)
    field = (i[:, None] + R * t[None, :] + r[:, None]) % F
    first = np.repeat(i[:, None], NT, axis=1)
    hq = np.arange(NHT)
    hidden = F * (hq // 2)[None, :] + (i[:, None] + HALFTURN * (hq % 2)[None, :]) % F
    chunk = hidden[:, :, None] * F + field[:, None, :]
    chunk = chunk.reshape(P, NHT, NT // UNIT, UNIT).transpose(0, 2, 1, 3)
    ih = np.arange(4 * HALFTURN) % HALFTURN

    ids = a["ids"].reshape(NB, 4, 4, F).transpose(3, 1, 0, 2).reshape(P, NB * 4)
    W0T = a["L0_rec_W0"].T
    W1T = a["L0_rec_W1"].T
    arrays = {
        "table": np.concatenate([a[f"tbl_{f}"] for f in range(F)], axis=0),
        "ids": ids,
        "field_row": field_row,
        "half_scale": half_scale,
        "w0_direct": W0T[first * F + field],
        "w0_mirror": W0T[field * F + first],
        "w0h_direct": W0T[ih * F + ih + HALFTURN],
        "w0h_mirror": W0T[(ih + HALFTURN) * F + ih],
        "w1": W1T[chunk].reshape(P, NHT * NT, O),
        "b0": a["L0_rec_b0"].reshape(O, 1),
        "b1": a["L0_rec_b1"].reshape(O, 1),
        "dense": a["dense_ctx"].T,
        "wtop1": a["W_top1"],
        "btop1": a["b_top1"].reshape(T1 // P, P).T,
        "wtop2": a["W_top2"].reshape(T1 // P, P, T2).transpose(1, 0, 2),
        "btop2": a["b_top2"].reshape(T2 // P, P).T,
        "wtop3": a["W_top3"].reshape(T2 // P, P).T,
    }
    arrays = {name: np.ascontiguousarray(v) for name, v in arrays.items()}

    nc = bacc.Bacc("TRN2", target_bir_lowering=False, num_devices=1)
    aps = {name: nc.dram_tensor(name, v.shape, mybir.dt.from_np(v.dtype), kind="ExternalInput").ap()
           for name, v in arrays.items()}
    y = nc.dram_tensor("y", (1, B), mybir.dt.from_np(f32), kind="ExternalOutput").ap()
    build_tower(nc, out=y, **aps)
    res = run_bass_kernel_spmd(nc, [arrays], core_ids=[0])
    return res.results[0]["y"].reshape(B, 1)
```

```python
import concourse.bass as bass
from concourse import mybir
from contextlib import ExitStack

VOCABS = [12500, 125000, 1250, 125000, 1000, 12500, 1000, 125000, 1000, 12500, 1250, 1250, 1250, 1000, 12500, 1000,
          1000, 12500, 1000, 1250, 1000, 1250, 1250, 1250, 1000, 1000, 1000, 1250, 12500, 1000, 1250, 1250]
P = 128
B = 1024
F = 32
D = 64
O = 128
HID = 64
CTX = 16
T1 = 512
T2 = 256

BS = 16
N = BS * D
NB = B // BS
BANK = 512
HALVES = N // BANK

R = 4
NT = 4
NHT = 4
RING = 2
UNITS0 = 1
UNITS1 = NHT
US = UNITS0 + UNITS1
HALFTURN = F // 2
CG = P // HALFTURN
CN = N // CG

FULL_STEP = [(1, 0), (0, 0), (1, 1), (1, 2), (1, 3)]
LAST_STEP = [(1, 0), (1, 1), (1, 2), (1, 3)]
L0_POS = FULL_STEP.index((0, 0))
TURN_AT = 2
TOP1_AT, TOP2_AT = 2, 3

SPLIT_FROM = 2
SPLIT_COLS = {(0, 0): 1 * BANK, (1, 0): 4 * BANK, (1, 1): 4 * BANK, (1, 2): 4 * BANK, (1, 3): 7 * BANK // 2}


def split_tiles(layer):
    return max(-(-cols // N) for unit, cols in SPLIT_COLS.items() if unit[0] == layer)


def split_slot(pos):
    return (UNITS0 + pos) % US


def unit_index(k, pos):
    return k * US + (UNITS0 + pos)


def build_tower(nc, table, ids, field_row, half_scale, w0_direct, w0_mirror, w0h_direct, w0h_mirror, w1,
                b0, b1, dense, wtop1, btop1, wtop2, btop2, wtop3, out):
    fp32 = mybir.dt.float32
    i32 = mybir.dt.int32
    f32r = mybir.dt.float32r
    ALU = mybir.AluOpType
    ACT = mybir.ActivationFunctionType

    ctx = ExitStack()
    with ctx:
        def sb(name, shape, dt=fp32):
            return ctx.enter_context(nc.sbuf_tensor(name, shape, dt))

        def pb(name, shape):
            return ctx.enter_context(nc.psum_tensor(name, shape, fp32))

        def sem(name):
            return ctx.enter_context(nc.semaphore(name))

        xs = nc.dram_tensor("xs", [NB, F + HALFTURN, N], fp32).ap()

        ids_sb = sb("ids_sb", [P, NB * 4], i32)
        row_of_field = sb("row_of_field", [P, 1], i32)
        rows = sb("rows", [P, NB * 4], i32)
        idx_now = [sb(f"idx_now{g}", [P, 4], i32) for g in range(2)]
        gathered = [sb(f"gathered{g}", [P, 4 * D]) for g in range(2)]
        base = sb("base", [P, 1, N])
        rot = [sb(f"rot{b}", [P, NT, N]) for b in range(2)]
        hid = [sb(f"hid{b}", [P, NHT, N]) for b in range(2)]
        SPLIT_TILES = RING * SPLIT_FROM
        prods = sb("prods", [P, SPLIT_TILES + US * (NT - SPLIT_FROM), N])
        whole_prod = [prods[:, SPLIT_FROM * u:SPLIT_FROM * (u + 1), :] for u in range(RING)]
        split_prod = [prods[:, SPLIT_TILES + (NT - SPLIT_FROM) * u:SPLIT_TILES + (NT - SPLIT_FROM) * (u + 1), :]
                      for u in range(US)]
        prod_hi = [sb(f"prod_hi{u}", [P, (NT - SPLIT_FROM) * N], f32r) for u in range(RING)]
        prod_lo = [sb(f"prod_lo{u}", [P, (NT - SPLIT_FROM) * N], f32r) for u in range(RING)]
        turn_a = [sb(f"turn_a{b}", [P, CN]) for b in range(2)]
        turn_b = [sb(f"turn_b{b}", [P, CN]) for b in range(2)]
        turn = sb("turn", [P, CN])
        turn_hi = [sb(f"turn_hi{b}", [P, CN], f32r) for b in range(2)]
        turn_lo = [sb(f"turn_lo{b}", [P, CN], f32r) for b in range(2)]
        stack = sb("stack", [4 * HALFTURN, N], f32r)
        act0 = [sb(f"act0_{b}", [HID, N]) for b in range(2)]
        sums0 = sb("sums0", [P, BS])
        sums1 = sb("sums1", [P, BS])
        w0_sb = sb("w0_sb", [P, NT, O])
        half_sb = sb("half_sb", [P, 1])
        w1_sb = sb("w1_sb", [P, NHT, NT, O])
        w0_hi = sb("w0_hi", [P, 1, split_tiles(0), O], f32r)
        w0_lo = sb("w0_lo", [P, 1, split_tiles(0), O], f32r)
        w1_hi = sb("w1_hi", [P, NHT, split_tiles(1), O], f32r)
        w1_lo = sb("w1_lo", [P, NHT, split_tiles(1), O], f32r)
        w_turn = sb("w_turn", [4 * HALFTURN, O])
        w_turn_m = sb("w_turn_m", [4 * HALFTURN, O])
        w_stack = sb("w_stack", [4 * HALFTURN, O], f32r)
        w_turn_hi = sb("w_turn_hi", [4 * HALFTURN, O], f32r)
        b0_sb = sb("b0_sb", [O, 1])
        b1_sb = sb("b1_sb", [O, 1])
        w0m_sb = prods[:, 0, 0:NT * O].rearrange("p (t o) -> p t o", t=NT)
        pooled0 = sb("pooled0", [P, B])
        pooled1 = sb("pooled1", [P, B])
        wt1a = hid[0][:, 0, 0:T1]
        wt1b = hid[0][:, 0, T1:2 * T1]
        bt1 = sb("bt1", [P, T1 // P])
        wt2 = hid[0][:, 1, :].rearrange("p (c n) -> p c n", n=T2)
        bt2 = sb("bt2", [P, T2 // P])
        wt3 = sb("wt3", [P, T2 // P])
        top1 = rot[0][:, 0:T1 // P, :]
        top2 = hid[0][:, 2:2 + T2 // P, :]
        y_sb = base[0:1, 0, :]

        out0 = pb("out0", [O, N])
        out1 = [pb(f"out1_{b}", [O, N]) for b in range(2)]
        spare = pb("spare", [P, 2, BANK])
        tops = [out0[:, 0:BANK], out0[:, BANK:2 * BANK], spare[:, 0, :], spare[:, 1, :],
                out1[(NB - 2) % 2][:, 0:BANK]]

        ids_in = sem("ids_in")
        rows_ready = sem("rows_ready")
        idx_ready = sem("idx_ready")
        gather_done = [sem(f"gather_done{g}") for g in range(2)]
        store_done = [sem(f"store_done{g}") for g in range(2)]
        w0_in = sem("w0_in")
        w1_in = sem("w1_in")
        wtop_in = sem("wtop_in")
        w0_summed = sem("w0_summed")
        w0_whole = sem("w0_whole")
        w0_ready = sem("w0_ready")
        w1_ready = sem("w1_ready")
        w0_hi_ready = sem("w0_hi_ready")
        w1_hi_ready = sem("w1_hi_ready")
        zeroed = sem("zeroed")
        head_loaded = [sem(f"head_loaded{b}") for b in range(2)]
        tail_loaded = [sem(f"tail_loaded{b}") for b in range(2)]
        whole_used = sem("whole_used")
        turn_loaded = [sem(f"turn_loaded{b}") for b in range(2)]
        turn_made = sem("turn_made")
        turn_hi_ready = sem("turn_hi_ready")
        turn_lo_ready = sem("turn_lo_ready")
        stack_loaded = sem("stack_loaded")
        stack_used = sem("stack_used")
        hid_loaded = [[sem(f"hid_loaded{b}_{h}") for h in range(NHT)] for b in range(2)]
        opening_ready = sem("opening_ready")
        prod_ready = sem("prod_ready")
        hi_ready = sem("hi_ready")
        lo_ready = sem("lo_ready")
        prod_used = sem("prod_used")
        act0_ready = sem("act0_ready")
        sums0_ready = sem("sums0_ready")
        sums1_ready = sem("sums1_ready")
        pooled0_done = sem("pooled0_done")
        pooled1_done = sem("pooled1_done")
        top_ready = sem("top_ready")
        top_read = sem("top_read")
        y_out = sem("y_out")

        HEAD_DMAS = 3
        TAIL_DMAS = 2
        HID_DMAS = [1, 2, 1, 2]

        TOP = [(layer, s, m) for s in range(2) for layer, tiles in ((1, T1 // P), (2, T2 // P), (3, 1))
               for m in range(tiles)]
        bank_of = {x: 4 if x[0] == 3 else x[2] for x in TOP}

        block = ctx.enter_context(nc.Block())

        def at(k, ph, j, ahead):
            return k + ahead, (ph + ahead) % 2, j + (ph + ahead) // 2 + 1

        def steps(eng, step):
            for k in range(2):
                step(k, k, 0)
            with eng.Fori(1, NB // 2 - 2) as j:
                step(j * 2, 0, j)
                step(j * 2 + 1, 1, j)
            for k in range(NB - 4, NB):
                step(k, k % 2, k // 2)

        def wait(eng, s, value):
            if not isinstance(value, int) or value > 0:
                eng.wait_ge(s, value)

        def work_out(eng, *values):
            for value in values:
                if not isinstance(value, int):
                    eng.compute_val(value)

        @block.sync
        def _(sp):
            sp.dma_start(ids_sb[:, :], ids).then_inc(ids_in, 16)
            sp.dma_start(row_of_field[:, :], field_row).then_inc(ids_in, 16)
            def store(k, g, nth):
                sp.wait_ge(gather_done[g], nth * 64)
                lower = xs[k, 0:F, :].rearrange("m (b c) -> (m b) c", c=4 * D)
                upper = xs[k, F:F + HALFTURN, :].rearrange("m (b c) -> (m b) c", c=4 * D)
                sp.dma_start(lower, gathered[g][:, :]).then_inc(store_done[g], 16)
                sp.dma_start(upper, gathered[g][0:HALFTURN * 4, :]).then_inc(store_done[g], 16)

            def load_turn(k, b, nth):
                work_out(sp, nth * 32, k - 1)
                sp.wait_ge(store_done[b], nth * 32)
                wait(sp, turn_made, k - 1)
                sp.dma_start(turn_a[b][:, :],
                             xs[k, 0:HALFTURN, :].rearrange("m (c n) -> (m c) n", n=CN)).then_inc(turn_loaded[b], 16)
                sp.dma_start(turn_b[b][:, :],
                             xs[k, HALFTURN:F, :].rearrange("m (c n) -> (m c) n", n=CN)).then_inc(turn_loaded[b], 16)

            def load_rot(k, b, t, loaded):
                first = xs[k, R * t:F, :]
                src = bass.AP(tensor=first.tensor, offset=first.offset, ap=[[N, F], [N, R], [1, N]])
                sp.dma_start(rot[b][:, t, :], src).then_inc(loaded[b], 16)

            def load_base(k, b, nth):
                done = 1 if isinstance(k, int) and k == 1 else unit_index(k - 2, L0_POS) + 1
                work_out(sp, done, nth * 32)
                wait(sp, prod_ready, done)
                sp.wait_ge(store_done[b], nth * 32)
                first = xs[k, 0:F, :]
                src = bass.AP(tensor=first.tensor, offset=first.offset, ap=[[N, F], [0, R], [1, N]])
                sp.dma_start(base[:, 0, :], src).then_inc(head_loaded[b], 16)

            def load_rots(k, b):
                wait(sp, prod_ready, unit_index(k - 1, 0))
                load_rot(k, b, 0, head_loaded)
                load_rot(k, b, 1, head_loaded)
                load_rot(k, b, 2, tail_loaded)
                load_rot(k, b, 3, tail_loaded)

            def spread_hidden(k, b):
                work_out(sp, k + 1, unit_index(k - 1, 0))
                sp.wait_ge(act0_ready, k + 1)
                wait(sp, prod_ready, unit_index(k - 1, 0))
                for h in range(NHT):
                    s, q = h // 2, h % 2
                    for dst, src, rows_ in (((0, 0, F),) if q == 0 else
                                            ((0, HALFTURN, HALFTURN), (HALFTURN, 0, HALFTURN))):
                        rows_sb = act0[b][F * s + src:F * s + src + rows_, :]
                        part = rows_sb.ap[0][0]
                        sp.dma_start(
                            hid[b][R * dst:R * (dst + rows_), h, :],
                            bass.AP(tensor=rows_sb.tensor, offset=rows_sb.offset, ap=[[part, rows_], [0, R], [1, N]]),
                        ).then_inc(hid_loaded[b][h], 16)

            def copy_stack(k, b):
                work_out(sp, k + 1, k)
                sp.wait_ge(turn_lo_ready, k + 1)
                wait(sp, stack_used, k)
                for g in range(4):
                    rows_of_part = stack[g * HALFTURN:(g + 1) * HALFTURN, :].bitcast(fp32)
                    sp.dma_start(rows_of_part.rearrange("m (c n) -> m c n", n=CN),
                                 (turn_hi, turn_lo)[g % 2][b][:, :].bitcast(fp32)).then_inc(stack_loaded, 16)

            for dst, src in ((w0_sb[:, :, :], w0_direct), (w0m_sb, w0_mirror), (w_turn[:, :], w0h_direct),
                             (w_turn_m[:, :], w0h_mirror), (half_sb[:, :], half_scale), (b0_sb[:, :], b0)):
                sp.dma_start(dst, src).then_inc(w0_in, 16)
            sp.dma_start(w1_sb[:, :, :, :], w1).then_inc(w1_in, 16)
            sp.dma_start(b1_sb[:, :], b1).then_inc(w1_in, 16)
            store(0, 0, 1)
            load_turn(0, 0, 1)
            load_base(0, 0, 1)
            load_rots(0, 0)
            copy_stack(0, 0)
            store(1, 1, 1)
            load_turn(1, 1, 1)
            load_base(1, 1, 1)
            load_rots(1, 1)
            copy_stack(1, 1)
            spread_hidden(0, 0)
            store(2, 0, 2)
            load_turn(2, 0, 2)
            sp.wait_ge(zeroed, 1)
            sp.dma_start(pooled0[0:CTX, :], dense).then_inc(wtop_in, 16)
            sp.dma_start(bt1[:, :], btop1).then_inc(wtop_in, 16)
            sp.dma_start(bt2[:, :], btop2).then_inc(wtop_in, 16)
            sp.dma_start(wt3[:, :], wtop3).then_inc(wtop_in, 16)

            def step(k, ph, j):
                last = k if isinstance(k, int) else 0
                if last + 3 < NB:
                    store(*at(k, ph, j, 3))
                    load_turn(*at(k, ph, j, 3))
                if last + 2 < NB:
                    load_base(*at(k, ph, j, 2))
                if last + 1 < NB:
                    spread_hidden(*at(k, ph, j, 1)[:2])
                if last + 2 < NB:
                    copy_stack(*at(k, ph, j, 2)[:2])
                    load_rots(*at(k, ph, j, 2)[:2])

            steps(sp, step)

            sp.wait_ge(zeroed, 2)
            sp.dma_start(wt1a[0:CTX, :], wtop1[HID + O:HID + O + CTX, :]).then_inc(wtop_in, 16)
            sp.dma_start(wt1a[HID:P, :], wtop1[0:HID, :]).then_inc(wtop_in, 16)
            sp.dma_start(wt1b, wtop1[HID:HID + O, :]).then_inc(wtop_in, 16)
            sp.dma_start(wt2, wtop2).then_inc(wtop_in, 16)
            sp.wait_ge(top_read, len(TOP))
            sp.dma_start(out, y_sb[:, :]).then_inc(y_out, 16)
            sp.wait_ge(y_out, 16)

        @block.gpsimd
        def _(pool):
            pool.wait_ge(ids_in, 32)
            nc.gpsimd.tensor_tensor(rows[:, :], ids_sb[:, :], row_of_field[:, 0:1].to_broadcast([P, NB * 4]),
                                    ALU.add).then_inc(rows_ready, 1)

            def pick(k, g):
                nc.gpsimd.tensor_copy(idx_now[g][:, :], rows[:, bass.ds(k * 4, 4)]).then_inc(idx_ready, 1)

            def gather(k, g, before, more=True):
                wait(pool, store_done[g], before * 32)
                if more:
                    wait(pool, gather_done[1 - g], (before + g) * 64)
                    pool.wait_ge(idx_ready, k + 1)
                    pick(k + 1, 1 - g)
                else:
                    pool.wait_ge(idx_ready, k + 1)
                for s in range(4):
                    nc.gpsimd.indirect_dma_start(
                        out=gathered[g][:, s * D:(s + 1) * D], out_offset=None, in_=table,
                        in_offset=bass.IndirectOffsetOnAxis(ap=idx_now[g][:, s:s + 1], axis=0),
                    ).then_inc(gather_done[g], 16)

            pool.wait_ge(rows_ready, 1)
            pick(0, 0)
            gather(0, 0, 0)
            gather(1, 1, 0)
            with pool.Fori(1, NB // 2 - 1) as j:
                gather(j * 2, 0, j)
                gather(j * 2 + 1, 1, j)
            gather(NB - 2, 0, NB // 2 - 1)
            gather(NB - 1, 1, NB // 2 - 1, more=False)

        @block.vector
        def _(dve):
            nc.vector.memset(pooled0[:, :], 0.0).then_inc(zeroed, 1)

            def make_turn(k, b, nth):
                dve.wait_ge(turn_loaded[b], nth * 32)
                wait(dve, turn_lo_ready, k)
                nc.vector.tensor_tensor(turn[:, :], turn_a[b][:, :], turn_b[b][:, :], ALU.mult).then_inc(turn_made, 1)

            def low_turn(k, b, nth):
                wait(dve, stack_loaded, (k - 1) * 64)
                dve.wait_ge(turn_hi_ready, k + 1)
                nc.vector.tensor_tensor(turn_lo[b][:, :], turn[:, :], turn_hi[b][:, :].bitcast(fp32),
                                        ALU.subtract).then_inc(turn_lo_ready, 1)

            def room(index):
                wait(dve, whole_used, index - RING + 1)
                wait(dve, lo_ready, index - US + 1)

            def product(index, slot, sslot, factor, tiles):
                room(index)
                whole, split = whole_prod[slot], split_prod[sslot]
                to_split = split.offset - whole.offset
                out_ap = bass.AP(tensor=whole.tensor, offset=whole.offset,
                                 ap=[whole.ap[0], [to_split, 2], [N, NT // 2], [1, N]])
                nc.vector.tensor_tensor(out_ap, tiles[:, :, :].rearrange("p (a t) n -> p a t n", a=2),
                                        factor.to_broadcast([P, NT, N]).rearrange("p (a t) n -> p a t n", a=2),
                                        ALU.mult).then_inc(prod_ready, 1)

            def layer0_product(index, slot, sslot, b, nth):
                room(index)
                for first, dst, loaded, dmas in ((0, whole_prod[slot], head_loaded, HEAD_DMAS),
                                                 (2, split_prod[sslot], tail_loaded, TAIL_DMAS)):
                    dve.wait_ge(loaded[b], nth * dmas * 16)
                    a = nc.vector.tensor_tensor(dst, rot[b][:, first:first + 2, :],
                                                base[:, 0:1, :].to_broadcast([P, 2, N]), ALU.mult)
                    if isinstance(index, int) and index == 0 and first == 0:
                        a.then_inc(opening_ready, 1)
                a.then_inc(prod_ready, 1)

            def low_part(index, slot, sslot, x):
                dve.wait_ge(hi_ready, index + 1)
                c = slice(0, SPLIT_COLS[x])
                nc.vector.tensor_tensor(prod_lo[slot][:, c], split_prod[sslot].rearrange("p t n -> p (t n)")[:, c],
                                        prod_hi[slot][:, c].bitcast(fp32), ALU.subtract).then_inc(lo_ready, 1)

            dve.wait_ge(w0_in, 16 * 6)
            nc.vector.tensor_tensor(w0_sb[:, :, :], w0_sb[:, :, :], w0m_sb, ALU.add).then_inc(w0_summed, 1)
            nc.vector.tensor_tensor(w_turn[:, :], w_turn[:, :], w_turn_m[:, :], ALU.add).then_inc(w0_summed, 1)
            dve.wait_ge(w0_summed, 2)
            nc.vector.tensor_scalar(w0_sb[:, 0, :], w0_sb[:, 0, :], half_sb[:, 0:1], None,
                                    ALU.mult).then_inc(w0_whole, 1)
            half = 2 * HALFTURN
            nc.vector.tensor_copy(w_turn_hi[:, :], w_turn[:, :]).then_inc(w0_whole, 1)
            nc.vector.tensor_copy(w_stack[0:half, :], w_turn[0:half, :]).then_inc(w0_ready, 1)
            dve.wait_ge(w0_whole, 2)
            nc.vector.tensor_tensor(w_stack[half:2 * half, :], w_turn[half:2 * half, :],
                                    w_turn_hi[half:2 * half, :].bitcast(fp32), ALU.subtract).then_inc(w0_ready, 1)
            dve.wait_ge(w0_hi_ready, 1)
            nc.vector.tensor_tensor(w0_lo[:, 0, :, :], w0_sb[:, SPLIT_FROM:SPLIT_FROM + split_tiles(0), :],
                                    w0_hi[:, 0, :, :].bitcast(fp32), ALU.subtract).then_inc(w0_ready, 1)
            dve.wait_ge(w1_hi_ready, 1)
            nc.vector.tensor_tensor(w1_lo[:, :, :, :], w1_sb[:, :, SPLIT_FROM:SPLIT_FROM + split_tiles(1), :],
                                    w1_hi[:, :, :, :].bitcast(fp32), ALU.subtract).then_inc(w1_ready, 1)

            make_turn(0, 0, 1)
            low_turn(0, 0, 1)
            layer0_product(0, 0, 0, 0, 1)
            low_part(0, 0, 0, (0, 0))
            make_turn(1, 1, 1)
            low_turn(1, 1, 1)

            def step(k, ph, j):
                number = k if isinstance(k, int) else 0
                first = isinstance(k, int) and k == 0
                order = FULL_STEP if number < NB - 1 else LAST_STEP
                _, b, nth = at(k, ph, j, 0)
                if order is LAST_STEP:
                    dve.wait_ge(prod_ready, unit_index(k, 0))
                    nc.vector.memset(wt1a, 0.0).then_inc(zeroed, 1)
                before = None if first else FULL_STEP[-1]
                for pos, x in enumerate(order):
                    index, slot = unit_index(k, pos), (UNITS0 + ph + pos) % RING
                    if x[0] == 1:
                        h = x[1]
                        dve.wait_ge(hid_loaded[b][h], nth * HID_DMAS[h] * 16)
                        product(index, slot, split_slot(pos), hid[b][:, h:h + 1, :], rot[b])
                    else:
                        layer0_product(index, slot, split_slot(pos), *at(k, ph, j, 1)[1:])
                    if before:
                        low_part(index - 1, 1 - slot, split_slot(pos - 1), before)
                    before = x
                    if pos == TURN_AT and number + 2 < NB:
                        make_turn(*at(k, ph, j, 2))
                    if pos == TURN_AT + 1 and number + 2 < NB:
                        low_turn(*at(k, ph, j, 2))
                if order is LAST_STEP:
                    low_part(index, slot, split_slot(pos), before)

            steps(dve, step)

        @block.tensor
        def _(pe):
            def split_in(x, t, h):
                before = ((t - SPLIT_FROM) * HALVES + h) * BANK
                return min(max(SPLIT_COLS[x] - before, 0), BANK) if t >= SPLIT_FROM else 0

            def add_up(acc, term, start, stop):
                h, first, w, z = term
                at_col = h * BANK + first
                return nc.tensor.matmul(acc[:, at_col:at_col + z.shape[-1]], w, z, start=start, stop=stop)

            def terms_of(x, slot, sslot):
                tiles = [whole_prod[slot][:, t, :] for t in range(SPLIT_FROM)]
                tiles += [split_prod[sslot][:, t, :] for t in range(NT - SPLIT_FROM)]
                layer, u = x
                w, w_hi, w_lo = ((w0_sb, w0_hi[:, 0, :, :], w0_lo[:, 0, :, :]),
                                 (w1_sb[:, u, :, :], w1_hi[:, u, :, :], w1_lo[:, u, :, :]))[layer]
                whole, parts = [], []
                for t in range(NT):
                    for h in range(HALVES):
                        cut = split_in(x, t, h)
                        if cut < BANK:
                            whole.append((h, cut, w[:, t, :], tiles[t][:, h * BANK + cut:(h + 1) * BANK]))
                for t in reversed(range(SPLIT_FROM, NT)):
                    u = t - SPLIT_FROM
                    for wp, z in ((w_hi, prod_hi[slot]), (w_hi, prod_lo[slot]), (w_lo, prod_hi[slot])):
                        for h in range(HALVES):
                            first, cut = (u * HALVES + h) * BANK, split_in(x, t, h)
                            if cut:
                                parts.append((h, 0, wp[:, u, :], z[:, first:first + cut]))
                return whole, parts

            def layer0_of_block0():
                whole, _ = terms_of((0, 0), 0, 0)
                early = SPLIT_FROM * HALVES
                pe.wait_ge(opening_ready, 1)
                for n, term in enumerate(whole[:early]):
                    add_up(out0, term, start=n < HALVES, stop=False)
                turn_pairs(0, start=False)
                pe.wait_ge(prod_ready, 1)
                for n, term in enumerate(whole[early:]):
                    mm = add_up(out0, term, start=False, stop=early + n == len(whole) - 1)
                mm.then_inc(whole_used, 1)
                split_part((0, 0), 0, 0, 0, out0)

            def whole_part(x, index, slot, sslot, acc):
                whole, parts = terms_of(x, slot, sslot)
                used = [term[0] for term in whole + parts]
                pe.wait_ge(prod_ready, index + 1)
                for n, term in enumerate(whole):
                    mm = add_up(acc, term, start=x == (1, 0) and term[0] not in used[:n],
                                stop=x == (0, 0) and term[0] not in used[n + 1:])
                mm.then_inc(whole_used, 1)

            def split_part(x, index, slot, sslot, acc):
                _, parts = terms_of(x, slot, sslot)
                used = [term[0] for term in parts]
                pe.wait_ge(lo_ready, index + 1)
                for n, term in enumerate(parts):
                    mm = add_up(acc, term, start=False,
                                stop=x in ((0, 0), (1, NHT - 1)) and term[0] not in used[n + 1:])
                mm.then_inc(prod_used, 1)

            def turn_pairs(k, start=True):
                pe.wait_ge(stack_loaded, (k + 1) * 64)
                wait(pe, sums0_ready, k)
                for h in range(HALVES):
                    mm = nc.tensor.matmul(out0[:, h * BANK:(h + 1) * BANK], w_stack[:, :],
                                          stack[:, h * BANK:(h + 1) * BANK], start=start, stop=False)
                mm.then_inc(stack_used, 1)

            pe.wait_ge(w0_ready, 3)
            layer0_of_block0()
            pe.wait_ge(w1_in, 32)
            pe.wait_ge(w1_ready, 1)

            def halves(s):
                return slice(s * BANK, (s + 1) * BANK)

            def free_bank(x):
                before = [n for n, y in enumerate(TOP[:TOP.index(x)]) if bank_of[y] == bank_of[x]]
                if before:
                    pe.wait_ge(top_read, before[-1] + 1)
                elif bank_of[x] < 2:
                    pe.wait_ge(sums0_ready, NB)
                elif bank_of[x] == 4:
                    pe.wait_ge(sums1_ready, NB - 1)

            def open_top1(s):
                pe.wait_ge(wtop_in, 16 * 8)
                pe.wait_ge(pooled0_done, NB * (s + 1) // 2)
                for m in (2, 3, 0, 1):
                    free_bank((1, s, m))
                    nc.tensor.matmul(tops[m], wt1a[:, m * P:(m + 1) * P], pooled0[:, halves(s)],
                                     start=True, stop=False)

            def top(s, layer):
                if layer == 1:
                    pe.wait_ge(pooled1_done, NB * (s + 1) // 2)
                    for m in range(T1 // P):
                        nc.tensor.matmul(tops[m], wt1b[:, m * P:(m + 1) * P], pooled1[:, halves(s)],
                                         start=False, stop=True).then_inc(top_ready, 1)
                    return
                terms = (T1 if layer == 2 else T2) // P
                for m in range(T2 // P if layer == 2 else 1):
                    x = (layer, s, m)
                    free_bank(x)
                    for c in range(terms):
                        pe.wait_ge(top_read, TOP.index((layer - 1, s, c)) + 1)
                        if layer == 2:
                            mm = nc.tensor.matmul(tops[bank_of[x]], wt2[:, c, m * P:(m + 1) * P],
                                                  top1[:, c, halves(s)], start=c == 0, stop=c == terms - 1)
                        else:
                            mm = nc.tensor.matmul(tops[bank_of[x]][0:1, :], wt3[:, c:c + 1],
                                                  top2[:, c, halves(s)], start=c == 0, stop=c == terms - 1)
                    mm.then_inc(top_ready, 1)

            def step(k, ph, j):
                number = k if isinstance(k, int) else 0
                order = FULL_STEP if number < NB - 1 else LAST_STEP
                _, b, _ = at(k, ph, j, 0)
                wait(pe, sums1_ready, k - 1)
                before = None if isinstance(k, int) and k == 0 else (FULL_STEP[-1], out1[1 - b])
                for pos, x in enumerate(order):
                    index, slot = unit_index(k, pos), (UNITS0 + ph + pos) % RING
                    acc = out1[b] if x[0] == 1 else out0
                    if x[0] == 0:
                        turn_pairs(k + 1)
                    whole_part(x, index, slot, split_slot(pos), acc)
                    if before:
                        split_part(before[0], index - 1, 1 - slot, split_slot(pos - 1), before[1])
                    before = (x, acc)
                    if order is LAST_STEP and pos == TOP1_AT:
                        open_top1(0)
                        top(0, 1)
                    if order is LAST_STEP and pos == TOP2_AT:
                        split_part(x, index, slot, split_slot(pos), acc)
                        top(0, 2)

            steps(pe, step)
            open_top1(1)
            top(0, 3)
            top(1, 1)
            top(1, 2)
            top(1, 3)

        @block.scalar
        def _(act):
            def high_part(index, slot, sslot, x):
                act.wait_ge(prod_ready, index + 1)
                wait(act, prod_used, index - RING + 1)
                c = slice(0, SPLIT_COLS[x])
                nc.scalar.copy(prod_hi[slot][:, c],
                               split_prod[sslot].rearrange("p t n -> p (t n)")[:, c]).then_inc(hi_ready, 1)

            def high_turn(k, b, nth):
                act.wait_ge(turn_made, k + 1)
                wait(act, stack_loaded, (k - 1) * 64)
                nc.scalar.copy(turn_hi[b][:, :], turn[:, :]).then_inc(turn_hi_ready, 1)

            def relu0(k, b, nth, summed):
                act.wait_ge(prod_used, summed)
                if not (isinstance(nth, int) and nth == 1):
                    for h in range(NHT):
                        act.wait_ge(hid_loaded[b][h], (nth - 1) * HID_DMAS[h] * 16)
                nc.scalar.activation(act0[b][0:HID, :], out0[0:HID, :], ACT.Relu,
                                     bias=b0_sb[0:HID, 0:1]).then_inc(act0_ready, 1)

            def pool0(k, b, first, last):
                if first == 0:
                    wait(act, pooled0_done, k)
                for s in range(first, last):
                    c = slice(s * D, (s + 1) * D)
                    a = nc.scalar.activation(out0[HID:P, c], out0[HID:P, c], ACT.Relu, bias=b0_sb[HID:P, 0:1],
                                             accum_out=sums0[HID:P, s:s + 1])
                if last == BS:
                    a.then_inc(sums0_ready, 1)
                    act.wait_ge(sums0_ready, k + 1)
                    nc.scalar.copy(pooled0[HID:P, bass.ds(k * BS, BS)], sums0[HID:P, :]).then_inc(pooled0_done, 1)

            def pool1(k, b, first, last, summed=None):
                if first == 0:
                    act.wait_ge(prod_used, summed)
                    wait(act, pooled1_done, k)
                for s in range(first, last):
                    c = slice(s * D, (s + 1) * D)
                    a = nc.scalar.activation(out1[b][:, c], out1[b][:, c], ACT.Relu, bias=b1_sb[:, 0:1],
                                             accum_out=sums1[:, s:s + 1])
                if last == BS:
                    a.then_inc(sums1_ready, 1)
                    act.wait_ge(sums1_ready, k + 1)
                    nc.scalar.copy(pooled1[:, bass.ds(k * BS, BS)], sums1[:, :]).then_inc(pooled1_done, 1)

            act.wait_ge(w0_whole, 2)
            nc.scalar.copy(w0_hi[:, 0, :, :],
                           w0_sb[:, SPLIT_FROM:SPLIT_FROM + split_tiles(0), :]).then_inc(w0_hi_ready, 1)
            act.wait_ge(w1_in, 32)
            nc.scalar.copy(w1_hi[:, :, :, :],
                           w1_sb[:, :, SPLIT_FROM:SPLIT_FROM + split_tiles(1), :]).then_inc(w1_hi_ready, 1)
            high_turn(0, 0, 1)
            high_part(0, 0, 0, (0, 0))
            high_turn(1, 1, 1)
            relu0(0, 0, 1, 1)
            pool0(0, 0, 0, BS)

            POOL1_AT = {1: (0, 8), 3: (8, 12), 4: (12, BS)}
            RELU0_AT = 2
            POOL0_AT = {2: (0, 6), 3: (6, 11), 4: (11, BS)}

            def step(k, ph, j):
                number = k if isinstance(k, int) else 0
                first = isinstance(k, int) and k == 0
                order = FULL_STEP if number < NB - 1 else LAST_STEP
                nk, nb, nnth = at(k, ph, j, 1)
                for pos, x in enumerate(order):
                    high_part(unit_index(k, pos), (UNITS0 + ph + pos) % RING, split_slot(pos), x)
                    if pos == TURN_AT and number + 2 < NB:
                        high_turn(*at(k, ph, j, 2))
                    if pos == RELU0_AT and order is FULL_STEP:
                        relu0(nk, nb, nnth, unit_index(k, L0_POS) + 1)
                    if pos in POOL1_AT and not first:
                        pool1(k - 1, nb, *POOL1_AT[pos], unit_index(k, 0))
                    if pos in POOL0_AT and order is FULL_STEP:
                        pool0(nk, nb, *POOL0_AT[pos])
                if order is LAST_STEP:
                    pool1(k - 1, nb, *POOL1_AT[US - 1], unit_index(k, 0))

            steps(act, step)

            act.wait_ge(wtop_in, 16 * 8)

            def top(s, layer):
                for n, x in enumerate(TOP):
                    if (x[0], x[1]) != (layer, s):
                        continue
                    m, cols = x[2], slice(s * BANK, (s + 1) * BANK)
                    act.wait_ge(top_ready, n + 1)
                    if layer == 3:
                        nc.scalar.copy(y_sb[0:1, cols], tops[bank_of[x]][0:1, :]).then_inc(top_read, 1)
                    else:
                        dst, bias = ((top1, bt1), (top2, bt2))[layer - 1]
                        nc.scalar.activation(dst[:, m, cols], tops[bank_of[x]], ACT.Relu,
                                             bias=bias[:, m:m + 1]).then_inc(top_read, 1)

            top(0, 1)
            pool1(NB - 1, (NB - 1) % 2, 0, BS, unit_index(NB - 1, len(LAST_STEP)))
            for s, layer in ((0, 2), (0, 3), (1, 1), (1, 2), (1, 3)):
                top(s, layer)


def kernel(**inputs):
    import numpy as np
    import concourse.bacc as bacc
    from concourse.bass_utils import run_bass_kernel_spmd

    f32 = np.dtype("float32")
    i32 = np.dtype("int32")
    a = {name: np.asarray(value) for name, value in inputs.items()}

    p = np.arange(P)
    i, r = p // R, p % R
    starts = np.concatenate([[0], np.cumsum(VOCABS)[:-1]]).astype(i32)
    field_row = starts[i].reshape(P, 1)
    half_scale = np.where(r == 0, 0.5, 1.0).astype(f32).reshape(P, 1)
    t = np.arange(NT)
    field = (i[:, None] + R * t[None, :] + r[:, None]) % F
    first = np.repeat(i[:, None], NT, axis=1)
    hq = np.arange(NHT)
    hidden = F * (hq // 2)[None, :] + (i[:, None] + HALFTURN * (hq % 2)[None, :]) % F
    chunk = hidden[:, :, None] * F + field[:, None, :]
    ih = np.arange(4 * HALFTURN) % HALFTURN

    ids = a["ids"].reshape(NB, 4, 4, F).transpose(3, 1, 0, 2).reshape(P, NB * 4)
    W0T = a["L0_rec_W0"].T
    W1T = a["L0_rec_W1"].T
    arrays = {
        "table": np.concatenate([a[f"tbl_{f}"] for f in range(F)], axis=0),
        "ids": ids,
        "field_row": field_row,
        "half_scale": half_scale,
        "w0_direct": W0T[first * F + field],
        "w0_mirror": W0T[field * F + first],
        "w0h_direct": W0T[ih * F + ih + HALFTURN],
        "w0h_mirror": W0T[(ih + HALFTURN) * F + ih],
        "w1": W1T[chunk],
        "b0": a["L0_rec_b0"].reshape(O, 1),
        "b1": a["L0_rec_b1"].reshape(O, 1),
        "dense": a["dense_ctx"].T,
        "wtop1": a["W_top1"],
        "btop1": a["b_top1"].reshape(T1 // P, P).T,
        "wtop2": a["W_top2"].reshape(T1 // P, P, T2).transpose(1, 0, 2),
        "btop2": a["b_top2"].reshape(T2 // P, P).T,
        "wtop3": a["W_top3"].reshape(T2 // P, P).T,
    }
    arrays = {name: np.ascontiguousarray(v) for name, v in arrays.items()}

    nc = bacc.Bacc("TRN2", target_bir_lowering=False, num_devices=1)
    aps = {name: nc.dram_tensor(name, v.shape, mybir.dt.from_np(v.dtype), kind="ExternalInput").ap()
           for name, v in arrays.items()}
    y = nc.dram_tensor("y", (1, B), mybir.dt.from_np(f32), kind="ExternalOutput").ap()
    build_tower(nc, out=y, **aps)
    res = run_bass_kernel_spmd(nc, [arrays], core_ids=[0])
    return res.results[0]["y"].reshape(B, 1)
```
